# Optimizing a Trainium2 kernel written in Bass

```python
import numpy as np
import jax
import jax.numpy as jnp

def _softmax(x, axis=-1):
    return jax.nn.softmax(x, axis=axis)

def _gelu(x):
    return jax.nn.gelu(x, approximate=True)

def _silu(x):
    return jax.nn.silu(x)

def _sigmoid(x):
    return jax.nn.sigmoid(x)

def _layernorm(x, axis=-1, eps=1e-05):
    m = jnp.mean(x, axis=axis, keepdims=True)
    v = jnp.var(x, axis=axis, keepdims=True)
    return (x - m) / jnp.sqrt(v + eps)

def _scatter_add(tgt, idx, src, axis=0):
    return tgt.at[idx].add(src)

def _segment_sum(src, seg, n):
    return jax.ops.segment_sum(src, seg, n)
kernel_name = 'mk_flamingo_gated_d1_seqx_r2_279a30'

def setup_inputs(seed: int=0):
    np.random.seed(seed)
    _w = jnp.asarray

    def _rec_inputs():
        import jax
        import jax.numpy as jnp
        _rk = jax.random.key(seed)
        x = -0.0002928 + 1 * jax.random.normal(jax.random.fold_in(_rk, 1), (8, 512, 512), jnp.float32)
        _lenS = 512 - jax.random.randint(jax.random.fold_in(_rk, 7), (8,), 0, max(1, 512 // 4) + 1, jnp.int32)
        _lenS2 = 512 - jax.random.randint(jax.random.fold_in(_rk, 8), (8,), 0, max(1, 512 // 4) + 1, jnp.int32)
        _ctx_1024P = jax.random.normal(jax.random.fold_in(_rk, 11), (8, 16, 512), jnp.float32)
        _ctx_1024c = jax.random.dirichlet(jax.random.fold_in(_rk, 511), 0.3 * jnp.ones((16,), jnp.float32), (8, 512))
        _ctx_1024t = jnp.einsum('bsk,bkd->bsd', _ctx_1024c, _ctx_1024P)
        _ctx_1024t = _ctx_1024t * jax.lax.rsqrt(jnp.mean(jnp.square(_ctx_1024t)) + 1e-12) * 0.953939
        ctx_1024 = -1.39393e-06 + 0.999914 * (_ctx_1024t + 0.3 * jax.random.normal(jax.random.fold_in(_rk, 611), (8, 512, 512), jnp.float32))
        _validS = jnp.arange(512)[None, :] < _lenS[:, None]
        _validS2 = jnp.arange(512)[None, :] < _lenS2[:, None]
        _causal = jnp.tril(jnp.ones((512, 512), dtype=bool))
        mask_SxS2_bk1 = jnp.broadcast_to(_validS2[0:1, :], (512, 512))
        _g = jax.random.normal(jax.random.fold_in(_rk, 9001), (2, 1), jnp.float32)
        _g = jnp.sign(_g) * jnp.maximum(jnp.abs(_g), 1.0) + (_g == 0) * 1.0
        g_xattn = _g[0]
        g_ffn = _g[1]
        return (x, ctx_1024, mask_SxS2_bk1, g_xattn, g_ffn)
    x, ctx_1024, mask_SxS2_bk1, g_xattn, g_ffn = _rec_inputs()

    def _L0_xattn_setup():
        import jax, jax.numpy as jnp
        import numpy as np
        EMBED_DIM = 512
        NUM_HEADS = 16
        HEAD_DIM = EMBED_DIM // NUM_HEADS
        key = jax.random.key(seed)
        ks = jax.random.split(key, 12)
        B, S, D = (2, 1024, EMBED_DIM)
        sc = 1.0 / np.sqrt(D)
        inp = {'query': jax.random.normal(ks[0], (B, S, D), jnp.float32), 'key': jax.random.normal(ks[1], (B, S, D), jnp.float32), 'value': jax.random.normal(ks[2], (B, S, D), jnp.float32), 'attn_mask': jnp.triu(jnp.ones((S, S), dtype=bool), k=1), 'q_w': jax.random.normal(ks[3], (D, D), jnp.float32) * sc, 'q_b': jnp.zeros((D,), jnp.float32), 'k_w': jax.random.normal(ks[4], (D, D), jnp.float32) * sc, 'k_b': jnp.zeros((D,), jnp.float32), 'v_w': jax.random.normal(ks[5], (D, D), jnp.float32) * sc, 'v_b': jnp.zeros((D,), jnp.float32), 'o_w': jax.random.normal(ks[6], (D, D), jnp.float32) * sc, 'o_b': jnp.zeros((D,), jnp.float32)}
        return inp
    _L0_xattn_all = _L0_xattn_setup()
    _L0_xattn_in = {k: v for k, v in _L0_xattn_all.items() if k in ('q_w', 'q_b', 'k_w', 'k_b', 'v_w', 'v_b', 'o_w', 'o_b')}
    del _L0_xattn_all

    def _L0_ffn_setup():
        import jax, jax.numpy as jnp
        import numpy as np
        DIM = 512

        def _reference_tuple_inner(x, W_r, W_k, W_v, mu_r, mu_k):
            B, T, C = x.shape
            x_prev = jnp.concatenate([jnp.zeros((B, 1, C), x.dtype), x[:, :-1, :]], axis=1)
            xr = mu_r * x + (1.0 - mu_r) * x_prev
            xk = mu_k * x + (1.0 - mu_k) * x_prev
            r = jax.nn.sigmoid(jnp.einsum('btc,dc->btd', xr, W_r))
            k = jnp.einsum('btc,dc->btd', xk, W_k)
            k_act = jnp.square(jax.nn.relu(k))
            out = r * jnp.einsum('btc,dc->btd', k_act, W_v)
            new_state = x[:, -1, :]
            return (out, new_state)
        key = jax.random.key(seed)
        ks = jax.random.split(key, 6)
        B, T, C = (8, 1024, DIM)
        x = jax.random.normal(ks[0], (B, T, C), dtype=jnp.float32)
        s = 1.0 / np.sqrt(C)
        W_r = jax.random.uniform(ks[1], (C, C), jnp.float32, -s, s)
        W_k = jax.random.uniform(ks[2], (C, C), jnp.float32, -s, s)
        W_v = jax.random.uniform(ks[3], (C, C), jnp.float32, -s, s)
        mu_r = jax.random.uniform(ks[4], (C,), jnp.float32)
        mu_k = jax.random.uniform(ks[5], (C,), jnp.float32)
        return {'x': x, 'W_r': W_r, 'W_k': W_k, 'W_v': W_v, 'mu_r': mu_r, 'mu_k': mu_k}
    _L0_ffn_all = _L0_ffn_setup()
    _L0_ffn_in = {k: v for k, v in _L0_ffn_all.items() if k in ('W_r', 'W_k', 'W_v', 'mu_r', 'mu_k')}
    del _L0_ffn_all
    return {'x': x, 'ctx_1024': ctx_1024, 'mask_SxS2_bk1': mask_SxS2_bk1, 'g_xattn': g_xattn, 'g_ffn': g_ffn, 'L0_xattn_q_w': _L0_xattn_in['q_w'], 'L0_xattn_q_b': _L0_xattn_in['q_b'], 'L0_xattn_k_w': _L0_xattn_in['k_w'], 'L0_xattn_k_b': _L0_xattn_in['k_b'], 'L0_xattn_v_w': _L0_xattn_in['v_w'], 'L0_xattn_v_b': _L0_xattn_in['v_b'], 'L0_xattn_o_w': _L0_xattn_in['o_w'], 'L0_xattn_o_b': _L0_xattn_in['o_b'], 'L0_ffn_W_r': _L0_ffn_in['W_r'], 'L0_ffn_W_k': _L0_ffn_in['W_k'], 'L0_ffn_W_v': _L0_ffn_in['W_v'], 'L0_ffn_mu_r': _L0_ffn_in['mu_r'], 'L0_ffn_mu_k': _L0_ffn_in['mu_k']}

def reference(x, ctx_1024, mask_SxS2_bk1, g_xattn, g_ffn, L0_xattn_q_w, L0_xattn_q_b, L0_xattn_k_w, L0_xattn_k_b, L0_xattn_v_w, L0_xattn_v_b, L0_xattn_o_w, L0_xattn_o_b, L0_ffn_W_r, L0_ffn_W_k, L0_ffn_W_v, L0_ffn_mu_r, L0_ffn_mu_k):
    import jax
    import jax.numpy as jnp

    def _L0_xattn_ref(query, key, value, attn_mask, q_w, q_b, k_w, k_b, v_w, v_b, o_w, o_b):
        import jax, jax.numpy as jnp
        import numpy as np
        EMBED_DIM = 512
        NUM_HEADS = 16
        HEAD_DIM = EMBED_DIM // NUM_HEADS
        B, S, D = query.shape
        H, hd = (NUM_HEADS, HEAD_DIM)

        def proj(x, w, b):
            y = jnp.einsum('bsd,ed->bse', x, w) + b
            return y.reshape(B, S, H, hd).transpose(0, 2, 1, 3)
        Q = proj(query, q_w, q_b)
        K = proj(key, k_w, k_b)
        V = proj(value, v_w, v_b)
        scores = jnp.einsum('bhqd,bhkd->bhqk', Q, K) / jnp.sqrt(jnp.float32(hd))
        scores = jnp.where(attn_mask, jnp.float32(-1000000000.0), scores)
        attn = jax.nn.softmax(scores, axis=-1)
        ctx = jnp.einsum('bhqk,bhkd->bhqd', attn, V)
        ctx = ctx.transpose(0, 2, 1, 3).reshape(B, S, D)
        out = jnp.einsum('bsd,ed->bse', ctx, o_w) + o_b
        return out

    def _L0_ffn_ref(x, W_r, W_k, W_v, mu_r, mu_k):
        import jax, jax.numpy as jnp
        import numpy as np
        DIM = 512

        def _reference_tuple_inner(x, W_r, W_k, W_v, mu_r, mu_k):
            B, T, C = x.shape
            x_prev = jnp.concatenate([jnp.zeros((B, 1, C), x.dtype), x[:, :-1, :]], axis=1)
            xr = mu_r * x + (1.0 - mu_r) * x_prev
            xk = mu_k * x + (1.0 - mu_k) * x_prev
            r = jax.nn.sigmoid(jnp.einsum('btc,dc->btd', xr, W_r))
            k = jnp.einsum('btc,dc->btd', xk, W_k)
            k_act = jnp.square(jax.nn.relu(k))
            out = r * jnp.einsum('btc,dc->btd', k_act, W_v)
            new_state = x[:, -1, :]
            return (out, new_state)
        return _reference_tuple_inner(x, W_r, W_k, W_v, mu_r, mu_k)[0]
    x = x + jnp.tanh(g_xattn[0]) * _L0_xattn_ref(_layernorm(x, axis=-1), ctx_1024, ctx_1024, mask_SxS2_bk1, L0_xattn_q_w, L0_xattn_q_b, L0_xattn_k_w, L0_xattn_k_b, L0_xattn_v_w, L0_xattn_v_b, L0_xattn_o_w, L0_xattn_o_b)
    x = x + jnp.tanh(g_ffn[0]) * _L0_ffn_ref(_layernorm(x, axis=-1), L0_ffn_W_r, L0_ffn_W_k, L0_ffn_W_v, L0_ffn_mu_r, L0_ffn_mu_k)
    return x

_drawn_inputs = setup_inputs


def setup_inputs(seed=0):
    import zlib

    import numpy as np

    out = dict(_drawn_inputs(seed))
    spreads = {'L0_xattn_q_b': (0.0, 0.505),
     'L0_xattn_k_b': (0.0, 0.8),
     'L0_xattn_v_b': (0.0, 0.1),
     'L0_xattn_o_b': (0.0, 0.1)}
    factors = {'L0_ffn_W_r': 3.332, 'L0_ffn_mu_r': 7.588}
    for name, (base, spread) in spreads.items():
        noise = np.random.default_rng([zlib.crc32(name.encode()), seed]).standard_normal(out[name].shape)
        drawn = base * np.exp(spread * noise) if base else spread * noise
        out[name] = jnp.asarray(drawn.astype(out[name].dtype))
    for name, factor in factors.items():
        out[name] = (out[name] * factor).astype(out[name].dtype)
    return out
```

```python
from contextlib import ExitStack

import concourse.bass as bass
from concourse import mybir

F32 = mybir.dt.float32
F32R = mybir.dt.float32r
BF16 = mybir.dt.bfloat16
U8 = mybir.dt.uint8
I32 = mybir.dt.int32
ALU = mybir.AluOpType
ACT = mybir.ActivationFunctionType

P = 128
B, S, D = 8, 512, 512
NH, HD = 16, 32
CH = D // P
TT = S // P
GH = P // HD
GROUPS = NH // GH
TILES = GH * TT
EPS = 1e-5
SCALE = 1.0 / float(HD) ** 0.5
MASKED = 2.0 ** 100
RSQRT_MAGIC = float(0x5F3759DF)
NEWTON = 3

PARTS = 3
END = TILES + 1


def parts(kind, n, *steps):
    return {step: [(kind, n, part)] for part, step in enumerate(steps)}


T_STEPS = (7, 8, 9, 10, 11, 12, 13, 16)
PE_SIDE = [
    parts("Q", 1, 0, 1, 2) | parts("K", 1, 3, 5, 7) | parts("V", 2, 10, 13, 16),
    parts("Q", 2, 0, 1, 2) | parts("K", 2, 3, 5, 7) | parts("V", 3, 10, 13, 16),
    parts("Q", 3, 0, 1, 2) | parts("K", 3, 3, 4, 6) | {step: [("T", n, 0)] for n, step in enumerate(T_STEPS)},
    parts("Q", 4, 0, 1, 2) | parts("K", 4, 3, 4, 6) | parts("V", 0, 8, 9, 10) | parts("V", 1, 12, 14, 16),
]


def out_side(lag, r_step):
    table = [{} for _ in range(GROUPS)]
    for c in range(GROUPS):
        for step, items in PE_SIDE[c].items():
            kind, n, part = items[0]
            if kind == "T" or part == PARTS - 1:
                table[c].setdefault(min(step + 1 + (lag if kind != "V" else 0), END), []).append((kind, n))
        table[c][r_step] = [("R", (c - 1) % GROUPS)] + table[c].get(r_step, [])
    return table


HI_STEP, LO_STEP = 1, 2
HI_SIDE, LO_SIDE = out_side(0, HI_STEP), out_side(1, LO_STEP)
EARLY = LO_STEP + 1
PROLOGUE = [("T", n) for n in (4, 5, 6, 7)] + [("K", 0)] + [("T", n) for n in range(4)] + [("Q", 0), ("V", 0), ("V", 1)]
NEXT_BATCH = [("T", n) for n in range(8)] + [("Q", 4), ("K", 4), ("V", 0), ("V", 1)]
ORDER = [item for c in range(GROUPS) for item in
         [i[:2] for step in range(END) for i in PE_SIDE[c].get(step, []) if i[2] == 0] + [("R", c)]]
ORDER_LAST = [item for item in ORDER if item not in NEXT_BATCH]
SIDE_BANKS = 3
SIDE_PER_BATCH = len(ORDER)
HI_PER_BATCH, HI_PROLOGUE = (len([i for i in items if i[0] != "V"]) for items in (ORDER, PROLOGUE))
assert SIDE_PER_BATCH % SIDE_BANKS == 0

SM_RING, P_RING, S_BANKS = 4, 4, 2
HEAD = 1
DMA_HEAD = 16
STACK_DMAS = 6
UNIT = 256
UM = UNIT // P


def build(nc, x, ctx_in, mask, g_xattn, g_ffn, wq, bq, wk, bk, wv, bv, wo, bo, wr, wkk, wvv, mur, muk, ident_d, out, ctx_dram):
    keep = ExitStack()
    stage1 = ExitStack()
    stage2 = ExitStack()

    def sem(name):
        return keep.enter_context(nc.semaphore(name))

    def sb(stack, name, shape, dt=F32):
        return stack.enter_context(nc.sbuf_tensor(name, shape, dt))

    with keep:
        banks = [keep.enter_context(nc.psum_tensor(f"bank{i}", [P, 512], F32)) for i in range(8)]
        ident = sb(keep, "ident", [P, P])
        gates = sb(keep, "gates", [P, 2])
        tg = sb(keep, "tg", [P, 2])
        bq_col = sb(keep, "bq_col", [P, CH])
        bq_neg = sb(keep, "bq_neg", [P, CH])
        bk_col = sb(keep, "bk_col", [P, CH])
        mur_col = sb(keep, "mur_col", [P, CH])
        muk_col = sb(keep, "muk_col", [P, CH])
        bv_row = sb(keep, "bv_row", [P, D])
        tgbo = sb(keep, "tgbo", [P, D])

        w1_hi = [sb(stage1, f"w{n}_hi", [P, CH, D], F32R) for n in "qkv"]
        w1_lo = [sb(stage1, f"w{n}_lo", [P, CH, D], F32R) for n in "qkv"]
        act_hi = [sb(stage1, f"{n}T_hi", [P, CH, S], F32R) for n in ("x", "c")]
        act_lo = [sb(stage1, f"{n}T_lo", [P, CH, S], F32R) for n in ("x", "c")]
        nat = [sb(stage1, f"{n}_nat", [P, TT, D]) for n in ("x", "c")]
        qk_hi = [sb(stage1, f"{n}_hi", [P, S], F32R) for n in "qk"]
        qk_lo = [sb(stage1, f"{n}_lo", [P, S], F32R) for n in "qk"]
        stack = [[sb(stage1, f"{n}_stack{s}", [3 * HD, GH, S], F32R) for n in "qk"] for s in range(2)]
        v_sb = sb(stage1, "v_sb", [P, TT, D])
        pT = sb(stage1, "pT", [P, GH, TT, S])
        neg_s = sb(stage1, "neg_s", [P, SM_RING, S])
        probs = sb(stage1, "probs", [P, P_RING, S])
        mask_big = sb(stage1, "mask_big", [P, TT, S], BF16)
        negmax = sb(stage1, "negmax", [P, TILES])
        den = sb(stage1, "den", [P, 2, TILES])
        rden = sb(stage1, "rden", [P, TILES])
        rden_rep = sb(stage1, "rden_rep", [P, TT, GH, HD])
        ctx_sb = sb(stage1, "ctx_sb", [P, 2, S])
        stats = sb(stage1, "stats", [P, TT, 6])
        mv = sb(stage1, "mv", [P, TT, 2])
        var_eps = sb(stage1, "var_eps", [P, TT])
        newton = sb(stage1, "newton", [P, TT])
        rstd = sb(stage1, "rstd", [P, TT])
        mask_u8 = probs[:].rearrange("p r k -> p (r k)").bitcast(U8)[:, 0:TT * S].rearrange("p (t k) -> p t k", t=TT)
        stage1.close()

        w2_hi = [sb(stage2, f"w2{n}_hi", [P, CH, D], F32R) for n in "okrv"]
        w2_lo = [sb(stage2, f"w2{n}_lo", [P, CH, D], F32R) for n in "okrv"]
        w2_raw = sb(stage2, "w2_raw", [P, 2, CH, D])
        c_raw = sb(stage2, "c_raw", [P, 2, CH, UNIT])
        x_in = sb(stage2, "x_in", [P, 2, UM, D])
        x1 = sb(stage2, "x1", [P, 2, UM, D])
        o_sb = sb(stage2, "o_sb", [P, 2, UM, D])
        c_hi = sb(stage2, "c_hi", [P, CH, UNIT], F32R)
        c_lo = sb(stage2, "c_lo", [P, CH, UNIT], F32R)
        xh = sb(stage2, "xh", [P, UM, D])
        xT = sb(stage2, "xT", [P, 2, CH, 1 + UNIT])
        diff = sb(stage2, "diff", [P, CH, UNIT])
        mix = [sb(stage2, f"mix_{n}", [P, CH, UNIT]) for n in "kr"]
        mix_hi = [sb(stage2, f"mix_{n}_hi", [P, CH, UNIT], F32R) for n in "kr"]
        mix_lo = [sb(stage2, f"mix_{n}_lo", [P, CH, UNIT], F32R) for n in "kr"]
        relu = sb(stage2, "relu", [P, UM, D])
        kact = sb(stage2, "kact", [P, UM, D])
        kact_hi = sb(stage2, "kact_hi", [P, CH, UNIT], F32R)
        kact_lo = sb(stage2, "kact_lo", [P, CH, UNIT], F32R)
        recept = sb(stage2, "recept", [P, UM, D])
        stats2 = sb(stage2, "stats2", [P, UM, 6])
        mv2 = sb(stage2, "mv2", [P, UM, 2])
        var_eps2 = sb(stage2, "var_eps2", [P, UM])
        newton2 = sb(stage2, "newton2", [P, UM])
        rstd2 = sb(stage2, "rstd2", [P, UM])
        stage2.close()

        s_bank, pt_bank, pv_bank, side_bank = banks[0:2], banks[2:4], banks[4], banks[5:8]
        k_bank, r_bank, v_bank, o_bank = banks[0:2], banks[2:4], banks[4:6], banks[6:8]

        small_ld, bias_ld, bv_ld = sem("small_ld"), sem("bias_ld"), sem("bv_ld")
        unused = sem("unused")
        ident_ld = sem("ident_ld")
        mask_ld = sem("mask_ld")
        w_ld = [sem(f"w_ld{n}") for n in range(3)]
        consts = sem("consts")
        mask_done = sem("mask_done")
        w_hi_done, w_lo_done = sem("w_hi_done"), sem("w_lo_done")
        x_ld, c_ld = sem("x_ld"), sem("c_ld")
        bn_done, mv_done, pool_chain, xhat_done = sem("bn_done"), sem("mv_done"), sem("pool_chain"), sem("xhat_done")
        side_mm, side_hi, side_done = sem("side_mm"), sem("side_hi"), sem("side_done")
        stacked = [sem(f"stacked_head{j}") for j in range(GH)]
        s_mm, s_min, p_exp, p_tr = sem("s_mm"), sem("s_min"), sem("p_exp"), sem("p_tr")
        pt_out = [sem("pt_out_dve"), sem("pt_out_act")]
        rden_calc, rden_ready = sem("rden_calc"), sem("rden_ready")
        ctx_st = [sem("ctx_st0"), sem("ctx_st1")]
        w2_ld = [sem("w2_ld0"), sem("w2_ld1")]
        w2_hi_done, w2_lo_done = sem("w2_hi_done"), sem("w2_lo_done")
        c2_ld, x2_ld = [sem("c2_ld0"), sem("c2_ld1")], [sem("x2_ld0"), sem("x2_ld1")]
        c2_hi, c2_lo, xb_done = sem("c2_hi"), sem("c2_lo"), sem("xb_done")
        o_mm, x1_done, bn2_done, mv2_done = sem("o_mm"), sem("x1_done"), sem("bn2_done"), sem("mv2_done")
        pool_chain2, xh_done, t_mm, xT_done, carry_done = (
            sem("pool_chain2"), sem("xh_done"), sem("t_mm"), sem("xT_done"), sem("carry_done"))
        diff_done, mix_done, mixhi_done, mixlo_done = sem("diff_done"), [sem("mixk"), sem("mixr")], [
            sem("mixk_hi"), sem("mixr_hi")], [sem("mixk_lo"), sem("mixr_lo")]
        k_mm, r_mm, v_mm = sem("k_mm"), sem("r_mm"), sem("v_mm")
        relu_done, kact_done, kacthi_done, kactlo_done, recept_done = (
            sem("relu_done"), sem("kact_done"), sem("kacthi_done"), sem("kactlo_done"), sem("recept_done"))
        y_done, o_done = sem("y_done"), sem("o_done")
        out_st = [sem("out_st0"), sem("out_st1")]

        def side_no(b, item):
            if b is None:
                return PROLOGUE.index(item)
            order = ORDER_LAST if isinstance(b, int) and b == B - 1 else ORDER
            return b * SIDE_PER_BATCH + len(PROLOGUE) + order.index(item)

        def side_bank_of(b, item):
            if b is None:
                return side_bank[PROLOGUE.index(item) % SIDE_BANKS]
            order = ORDER_LAST if isinstance(b, int) and b == B - 1 else ORDER
            return side_bank[(len(PROLOGUE) + order.index(item)) % SIDE_BANKS]

        def hi_no(b, item):
            if b is None:
                return PROLOGUE.index(item)
            order = [i for i in (ORDER_LAST if isinstance(b, int) and b == B - 1 else ORDER) if i[0] != "V"]
            return b * HI_PER_BATCH + HI_PROLOGUE + order.index(item)

        def done(number):
            return number + 1 + SIDE_BANKS

        def listed(table, b, c, step):
            return [i for i in table[c].get(step, []) if not (is_last(b) and i[:2] in NEXT_BATCH)
                    and not (c == 0 and i[:2] == ("R", GROUPS - 1))]

        def previous_r(b, c):
            return done(side_no(b, ("R", c - 1))) if c else b * SIDE_PER_BATCH + len(PROLOGUE) + SIDE_BANKS

        def is_last(b):
            return isinstance(b, int) and b == B - 1

        def tile_no(b, c, i):
            return b * (GROUPS * TILES) + (c * TILES + i)

        def where(c, i):
            c, i = c + i // TILES, i % TILES
            return c % 2, i // TT, i % TT

        def blocks(bank):
            return bank[:].rearrange("p (a t) -> p a t", a=TT)

        def apart(engine):
            engine.sem_inc(unused, 1)

        CHAIN = 3 + 4 * NEWTON

        block = keep.enter_context(nc.Block())

        @block.sync
        def _(sp):
            def load_rows(which, rows, b):
                sp.dma_start(nat[which][:], rows[bass.ds(b * S, S), :].rearrange("(t p) c -> p t c", p=P)).then_inc(
                    (x_ld, c_ld)[which], 16)

            def load_w(n, w):
                sp.dma_start(pT[:, n, :, :], w.rearrange("(a p) e -> p a e", p=P)).then_inc(w_ld[n], 16)

            sp.dma_start(ident[:], ident_d).then_inc(ident_ld, 16)
            load_rows(1, ctx_in, 0)
            load_rows(0, x, 0)
            load_w(1, wk)
            for t, a in ((bq_col, bq), (bk_col, bk)):
                sp.dma_start(t[:], a).then_inc(bias_ld, 16)
            load_w(0, wq)
            load_w(2, wv)
            sp.dma_start(mask_u8, mask.rearrange("(t p) k -> p t k", p=P)).then_inc(mask_ld, 16)
            sp.dma_start(bv_row[:], bv.to_broadcast([P, D])).then_inc(bv_ld, 16)
            for t, a in ((mur_col, mur), (muk_col, muk)):
                sp.dma_start(t[:], a).then_inc(small_ld, 16)
            sp.dma_start(gates[:, 0:1], g_xattn.to_broadcast([P, 1])).then_inc(small_ld, 16)
            sp.dma_start(gates[:, 1:2], g_ffn.to_broadcast([P, 1])).then_inc(small_ld, 16)
            sp.dma_start(tgbo[:], bo.to_broadcast([P, D])).then_inc(small_ld, 16)

            def stack_rows(b, kind, n, bands, source, heads=range(GH)):
                dst = stack[n % 2]["QK".index(kind)]
                for j in heads:
                    for band in bands:
                        sp.dma_start(dst[HD * band:HD * (band + 1), j, :].bitcast(F32),
                                     source[HD * j:HD * (j + 1), :].bitcast(F32)).then_inc(stacked[j], 16)

            def stack_group(b, kind, n):
                if kind == "Q":
                    sp.wait_ge(side_hi, hi_no(b, (kind, n)) + 1)
                    apart(sp)
                    stack_rows(b, kind, n, (0, 1), qk_hi[0])
                sp.wait_ge(side_done, done(side_no(b, (kind, n))))
                apart(sp)
                if kind == "Q":
                    stack_rows(b, kind, n, (2,), qk_lo[0])
                else:
                    for j in range(GH):
                        stack_rows(b, kind, n, (0, 2), qk_hi[1], (j,))
                        stack_rows(b, kind, n, (1,), qk_lo[1], (j,))

            stack_group(None, "K", 0)
            stack_group(None, "Q", 0)

            def batch(b):
                for c in range(GROUPS):
                    for step in range(END + 1):
                        for kind, n in listed(LO_SIDE, b, c, step) + [("R", c)] * (c == GROUPS - 1 and step == END):
                            if kind == "Q":
                                sp.wait_ge(s_mm, tile_no(b, c, 0) + HEAD)
                                apart(sp)
                            if kind in "QK":
                                stack_group(b, kind, n)
                            if kind == "R":
                                sp.wait_ge(side_done, done(side_no(b, (kind, n))))
                                apart(sp)
                                sp.dma_start(ctx_dram[bass.ds(b * D + n * P, P), :], ctx_sb[:, n % 2, :]).then_inc(
                                    ctx_st[n % 2], 16)
                    if c == 0 and not is_last(b):
                        sp.wait_ge(side_mm, b * SIDE_PER_BATCH + len(PROLOGUE))
                        apart(sp)
                        load_rows(0, x, b + 1)
                        load_rows(1, ctx_in, b + 1)
                    if c == 2 and is_last(b):
                        sp.wait_ge(side_mm, side_no(b, ("K", 3)) + 1)
                        apart(sp)
                        for n, w in enumerate((wo, wkk, wr, wvv)):
                            if n >= 2:
                                sp.wait_ge(w2_lo_done, n - 1)
                            sp.dma_start(w2_raw[:, n % 2], w.rearrange("(a p) e -> p a e", p=P)).then_inc(w2_ld[n % 2], 16)

            with sp.Fori(0, B - 1) as b:
                batch(b)
            batch(B - 1)

            for s in range(2):
                sp.wait_ge(ctx_st[s], 16 * 2 * B + DMA_HEAD)

            def load_unit(b, h):
                sp.dma_start(c_raw[:, h], ctx_dram[bass.ds(b * D, D), :].rearrange("(a p) t -> p a t", p=P)[
                    :, :, h * UNIT:(h + 1) * UNIT]).then_inc(c2_ld[h], 16)
                sp.dma_start(x_in[:, h], x[bass.ds(b * S + h * UNIT, UNIT), :].rearrange(
                    "(m p) c -> p m c", p=P)).then_inc(x2_ld[h], 16)

            load_unit(0, 0)
            load_unit(0, 1)

            def step2(b, h):
                if not is_last(b):
                    sp.wait_ge(c2_lo, b * 2 + h + 1)
                    apart(sp)
                    sp.wait_ge(x1_done, (b * 2 + h + 1) * UM)
                    apart(sp)
                    load_unit(b + 1, h)
                sp.wait_ge(o_done, b * 2 + h + 1 + HEAD)
                apart(sp)
                sp.dma_start(out[bass.ds(b * S + h * UNIT, UNIT), :].rearrange("(m p) c -> p m c", p=P),
                             o_sb[:, h]).then_inc(out_st[h], 16)

            with sp.Fori(0, B - 1) as b:
                step2(b, 0)
                step2(b, 1)
            step2(B - 1, 0)
            step2(B - 1, 1)
            for s in range(2):
                sp.wait_ge(out_st[s], 16 * B + DMA_HEAD)

        @block.tensor
        def _(pe):
            def one_term(part, dst, w_hi, w_lo, r_hi, r_lo, lhs, rhs):
                left, right = ((w_hi, r_lo), (w_lo, r_hi), (w_hi, r_hi))[part]
                for a in range(CH):
                    mm = nc.tensor.matmul(dst, lhs(left, a), rhs(right, a), start=(part == 0 and a == 0),
                                          stop=(part == PARTS - 1 and a == CH - 1))
                return mm

            def three_terms(*operands):
                for part in range(PARTS):
                    mm = one_term(part, *operands)
                return mm

            def side(b, kind, n, part):
                item = (kind, n)
                bank = side_bank_of(b, item)
                if part == 0:
                    pe.wait_ge(side_done, side_no(b, item) + 1)
                if kind == "T":
                    of = 0 if b is None else b + 1
                    if n < TT:
                        pe.wait_ge(xhat_done, of * TT + n + 1)
                    else:
                        pe.wait_ge(c_ld, of * 16 + 16)
                    rows = nat[n // TT][:, n % TT, :]
                    for a in range(CH):
                        mm = nc.tensor.transpose(bank[:, a * P:(a + 1) * P], rows[:, a * P:(a + 1) * P], ident[:])
                if kind in "QK":
                    which = "QK".index(kind)
                    if n in (0, 4) and part == 0:
                        pe.wait_ge(side_done, done(side_no(b, ("T", TT * which + TT - 1))))
                    cols = slice((n % 4) * P, (n % 4 + 1) * P)
                    mm = one_term(part, bank[:], w1_hi[which], w1_lo[which], act_hi[which], act_lo[which],
                                  lambda w, a: w[:, a, cols], lambda r, a: r[:, a, :])
                if kind == "V":
                    share = 2 * PARTS * CH // PARTS
                    for at in range(part * share, (part + 1) * share):
                        k, term, a = at // (PARTS * CH), at // CH % PARTS, at % CH
                        keys = 2 * (n % 2) + k
                        left, right = ((act_hi[1], w1_lo[2]), (act_lo[1], w1_hi[2]), (act_hi[1], w1_hi[2]))[term]
                        mm = nc.tensor.matmul(bank[:, k * UNIT:(k + 1) * UNIT], left[:, a, keys * P:(keys + 1) * P],
                                              right[:, a, n // 2 * UNIT:(n // 2 + 1) * UNIT],
                                              start=(term == 0 and a == 0), stop=(term == PARTS - 1 and a == CH - 1))
                if kind == "R":
                    pe.wait_ge(rden_ready, b * GROUPS + n + 1 + HEAD)
                    for q in range(TT):
                        mm = nc.tensor.transpose(bank[:, q * P:(q + 1) * P],
                                                 rden_rep[:, q].rearrange("p j d -> p (j d)"), ident[:])
                if kind in "TR" or part == PARTS - 1:
                    mm.then_inc(side_mm, 1)

            def scores(b, c, i):
                slot, j, q = where(c, i)
                if i % TT == 0:
                    pe.wait_ge(stacked[j], (b * GROUPS + c + i // TILES + 1) * STACK_DMAS * 16)
                pe.wait_ge(s_min, tile_no(b, c, i) + 1)
                nc.tensor.matmul(s_bank[i % S_BANKS][:], stack[slot][0][:, j, q * P:(q + 1) * P],
                                 stack[slot][1][:, j, :], start=True, stop=True).then_inc(s_mm, 1)

            def transpose_probs(b, c, i):
                pe.wait_ge(p_exp, tile_no(b, c, i) + 1 + SM_RING)
                pe.wait_ge(pt_out[i % 2], b * (GROUPS * TILES // 2) + (c * TILES + i) // 2 + HEAD)
                for a in range(TT):
                    mm = nc.tensor.transpose(pt_bank[i % 2][:, a * P:(a + 1) * P],
                                             probs[:, i % P_RING, a * P:(a + 1) * P], ident[:])
                mm.then_inc(p_tr, 1)

            def context(b, c):
                for s in range(2):
                    pe.wait_ge(pt_out[s], (b * GROUPS + c + 1) * (TILES // 2) + HEAD)
                pe.wait_ge(side_done, previous_r(b, c))
                for a in range(TT):
                    for j in range(GH):
                        head = c * GH + j
                        nc.tensor.matmul(pv_bank[j * HD:(j + 1) * HD, :], v_sb[:, a, head * HD:(head + 1) * HD],
                                         pT[:, j, a, :], start=(a == 0), stop=(a == TT - 1))

            pe.wait_ge(ident_ld, 16)
            for kind, n in PROLOGUE:
                if kind != "T":
                    pe.wait_ge(w_lo_done, 1 + "KQV".index(kind))
                for part in range(1 if kind == "T" else PARTS):
                    side(None, kind, n, part)
            for i in range(2):
                scores(0, 0, i)

            def batch(b):
                for c in range(GROUPS):
                    for i in range(TILES):
                        if not (is_last(b) and c == GROUPS - 1 and i + 2 >= TILES):
                            scores(b, c, i + 2)
                        for kind, n, part in listed(PE_SIDE, b, c, i):
                            side(b, kind, n, part)
                        transpose_probs(b, c, i)
                    for kind, n, part in listed(PE_SIDE, b, c, TILES):
                        side(b, kind, n, part)
                    context(b, c)
                    side(b, "R", c, 0)

            with pe.Fori(0, B - 1) as b:
                batch(b)
            batch(B - 1)

            def o_proj(b, h):
                u = b * 2 + h
                pe.wait_ge(c2_lo, u + 1)
                pe.wait_ge(x1_done, u * UM)
                for m in range(UM):
                    three_terms(o_bank[m][:], c_hi, c_lo, w2_hi[0], w2_lo[0],
                                lambda w, a: w[:, a, m * P:(m + 1) * P], lambda r, a: r[:, a, :]).then_inc(o_mm, 1)

            def transposes(b, h):
                u = b * 2 + h
                pe.wait_ge(kact_done, u * UM + HEAD)
                for m in range(UM):
                    pe.wait_ge(xh_done, u * UM + m + 1)
                    for a in range(CH):
                        mm = nc.tensor.transpose(k_bank[m][:, a * P:(a + 1) * P], xh[:, m, a * P:(a + 1) * P], ident[:])
                    mm.then_inc(t_mm, 1)

            def k_proj(b, h):
                pe.wait_ge(mixlo_done[0], b * 2 + h + 1)
                for m in range(UM):
                    for half in range(2):
                        n = 2 * m + half
                        mm = three_terms(k_bank[m][:, half * UNIT:(half + 1) * UNIT], w2_hi[1], w2_lo[1],
                                         mix_hi[0], mix_lo[0], lambda w, a: w[:, a, n * P:(n + 1) * P],
                                         lambda r, a: r[:, a, :])
                    mm.then_inc(k_mm, 1)

            def r_proj(b, h):
                u = b * 2 + h
                pe.wait_ge(mixlo_done[1], u + 1)
                pe.wait_ge(recept_done, u * UM + HEAD)
                for m in range(UM):
                    three_terms(r_bank[m][:], mix_hi[1], mix_lo[1], w2_hi[2], w2_lo[2],
                                lambda w, a: w[:, a, m * P:(m + 1) * P], lambda r, a: r[:, a, :]).then_inc(r_mm, 1)

            def v_proj(b, h):
                u = b * 2 + h
                pe.wait_ge(kactlo_done, u + 1 + HEAD)
                pe.wait_ge(y_done, u * UM + HEAD)
                for m in range(UM):
                    three_terms(v_bank[m][:], kact_hi, kact_lo, w2_hi[3], w2_lo[3],
                                lambda w, a: w[:, a, m * P:(m + 1) * P], lambda r, a: r[:, a, :]).then_inc(v_mm, 1)

            pe.wait_ge(w2_lo_done, 4)
            o_proj(0, 0)
            o_proj(0, 1)
            transposes(0, 0)

            def step2(b, h):
                k_proj(b, h)
                r_proj(b, h)
                if h == 0:
                    transposes(b, 1)
                elif not is_last(b):
                    transposes(b + 1, 0)
                v_proj(b, h)
                if not is_last(b):
                    o_proj(b + 1, h)

            with pe.Fori(0, B - 1) as b:
                step2(b, 0)
                step2(b, 1)
            step2(B - 1, 0)
            step2(B - 1, 1)

        @block.scalar
        def _(act):
            def split_w(n):
                act.wait_ge(w_ld[n], 16)
                nc.scalar.mul(w1_hi[n][:], pT[:, n], -SCALE if n == 0 else 1.0).then_inc(w_hi_done, 1)

            def side(b, kind, n):
                item = (kind, n)
                bank = side_bank_of(b, item)
                if kind == "V":
                    return
                if kind == "Q" and n:
                    for copied in stacked:
                        act.wait_ge(copied, (b * GROUPS + n) * STACK_DMAS * 16)
                if kind == "R":
                    act.wait_ge(ctx_st[n % 2], (b * 2 + n // 2) * 16 + DMA_HEAD)
                act.wait_ge(side_mm, side_no(b, item) + 1)
                if kind == "T":
                    t = n % TT
                    nc.scalar.copy(act_hi[n // TT][:, :, t * P:(t + 1) * P], blocks(bank)).then_inc(side_hi, 1)
                if kind in "QK":
                    which = "QK".index(kind)
                    bias = (bq_neg, bk_col)[which][:, n % 4:n % 4 + 1]
                    nc.scalar.activation(qk_hi[which][:], bank[:], ACT.Identity, bias=bias).then_inc(side_hi, 1)
                if kind == "R":
                    nc.scalar.copy(ctx_sb[:, n % 2, :], bank[:]).then_inc(side_hi, 1)

            def exp(b, c, i):
                if i == TILES:
                    act.wait_ge(rden_ready, b * GROUPS + c + HEAD)
                act.wait_ge(s_min, tile_no(b, c, i) + 1 + S_BANKS)
                act.wait_ge(p_tr, tile_no(b, c, i) + 1)
                g = (c + i // TILES) % 2
                k = i % TILES
                nc.scalar.activation(probs[:, i % P_RING, :], neg_s[:, i % SM_RING, :], ACT.Exp,
                                     bias=negmax[:, k:k + 1], scale=-1.0,
                                     accum_out=den[:, g, k:k + 1]).then_inc(p_exp, 1)

            def probs_out(b, c, i):
                _, j, q = where(c, i)
                act.wait_ge(p_tr, tile_no(b, c, i) + 1 + P_RING)
                nc.scalar.copy(pT[:, j, :, q * P:(q + 1) * P], blocks(pt_bank[i % 2])).then_inc(pt_out[1], 1)

            for kind, n in PROLOGUE:
                if kind == "K":
                    split_w(1)
                    act.wait_ge(bias_ld, 16 * 2)
                    nc.scalar.mul(bq_neg[:], bq_col[:], -SCALE).then_inc(consts, 1)
                    split_w(0)
                    split_w(2)
                if kind == "Q":
                    act.wait_ge(consts, 1)
                side(None, kind, n)
                if kind == "Q":
                    act.wait_ge(small_ld, 16 * 5)
                    nc.scalar.activation(tg[:], gates[:], ACT.Tanh).then_inc(consts, 1)
            exp(0, 0, 0)

            def tile_step(b, c, i):
                if not (is_last(b) and c == GROUPS - 1 and i + 1 >= TILES):
                    exp(b, c, i + 1)
                for kind, n in listed(HI_SIDE, b, c, i):
                    side(b, kind, n)
                if i % 2:
                    probs_out(b, c, i)

            def early_steps(b):
                for i in range(EARLY):
                    tile_step(b, 0, i)
                    if i == HI_STEP and not isinstance(b, int):
                        side(b - 1, "R", GROUPS - 1)

            def batch(b):
                for c in range(GROUPS):
                    for i in range(EARLY if c == 0 else 0, TILES):
                        tile_step(b, c, i)
                        if is_last(b) and c == GROUPS - 1 and i in (2, 5, 8, 11):
                            n = (i - 2) // 3
                            act.wait_ge(w2_ld[n % 2], 16 * (n // 2 + 1))
                            nc.scalar.copy(w2_hi[n][:], w2_raw[:, n % 2]).then_inc(w2_hi_done, 1)
                    for kind, n in listed(HI_SIDE, b, c, END):
                        side(b, kind, n)
                if not is_last(b):
                    early_steps(b + 1)

            early_steps(0)
            with act.Fori(0, B - 1) as b:
                batch(b)
            batch(B - 1)
            side(B - 1, "R", GROUPS - 1)

            def context_hi(b, h):
                act.wait_ge(c2_ld[h], b * 16 + 16)
                act.wait_ge(o_mm, (b * 2 + h) * UM)
                nc.scalar.copy(c_hi[:], c_raw[:, h]).then_inc(c2_hi, 1)

            def xT_out(b, h):
                u = b * 2 + h
                if h == 1:
                    act.wait_ge(xT_done, u * UM)
                    nc.scalar.copy(xT[:, 1, :, 0:1], xT[:, 0, :, UNIT:UNIT + 1]).then_inc(carry_done, 1)
                for m in range(UM):
                    act.wait_ge(t_mm, u * UM + m + 1)
                    nc.scalar.copy(xT[:, h, :, 1 + m * P:1 + (m + 1) * P], blocks(k_bank[m])).then_inc(xT_done, 1)

            def mixed_hi(b, h, n):
                act.wait_ge(mix_done[n], (b * 2 + h + 1) * CH)
                nc.scalar.copy(mix_hi[n][:], mix[n][:]).then_inc(mixhi_done[n], 1)

            def step2(b, h):
                u = b * 2 + h
                for m in range(UM):
                    act.wait_ge(kact_done, u * UM + HEAD)
                    act.wait_ge(k_mm, u * UM + m + 1)
                    nc.scalar.activation(relu[:, m], k_bank[m][:], ACT.Relu).then_inc(relu_done, 1)
                act.wait_ge(kact_done, (u + 1) * UM + HEAD)
                nc.scalar.copy(kact_hi[:].rearrange("p a t -> p (a t)"),
                               kact[:].rearrange("p m d -> p (m d)")).then_inc(kacthi_done, 1)
                if not is_last(b):
                    context_hi(b + 1, h)
                act.wait_ge(y_done, u * UM + HEAD)
                for m in range(UM):
                    act.wait_ge(r_mm, u * UM + m + 1)
                    nc.scalar.activation(recept[:, m], r_bank[m][:], ACT.Sigmoid).then_inc(recept_done, 1)
                if not (h and is_last(b)):
                    nb, nh = (b, 1) if h == 0 else (b + 1, 0)
                    xT_out(nb, nh)
                    mixed_hi(nb, nh, 0)
                    mixed_hi(nb, nh, 1)

            context_hi(0, 0)
            context_hi(0, 1)
            xT_out(0, 0)
            mixed_hi(0, 0, 0)
            mixed_hi(0, 0, 1)
            with act.Fori(0, B - 1) as b:
                step2(b, 0)
                step2(b, 1)
            step2(B - 1, 0)
            step2(B - 1, 1)

        @block.vector
        def _(dve):
            def split_w(n):
                dve.wait_ge(w_hi_done, 1 + (1, 0, 2).index(n))
                nc.vector.scalar_tensor_tensor(out=w1_lo[n][:], in0=pT[:, n], scalar=-SCALE if n == 0 else 1.0,
                                               in1=w1_hi[n][:], op0=ALU.mult, op1=ALU.subtract).then_inc(w_lo_done, 1)

            def layer_stats(b):
                dve.wait_ge(x_ld, b * 16 + 16)
                dve.wait_ge(mv_done, b * TT)
                dve.wait_ge(xhat_done, b * TT)
                for t in range(TT):
                    nc.vector.bn_stats(stats[:, t, :], nat[0][:, t, :]).then_inc(bn_done, 1)
                for t in range(TT):
                    dve.wait_ge(bn_done, b * TT + t + 1)
                    apart(dve)
                    nc.vector.bn_aggr(mv[:, t, :], stats[:, t, :]).then_inc(mv_done, 1)

            def side(b, kind, n):
                item = (kind, n)
                bank = side_bank_of(b, item)
                if kind == "V":
                    dve.wait_ge(side_mm, side_no(b, item) + 1)
                    cols = slice(n // 2 * UNIT, (n // 2 + 1) * UNIT)
                    nc.vector.tensor_tensor(v_sb[:, 2 * (n % 2):2 * (n % 2) + 2, cols],
                                            bank[:].rearrange("p (k e) -> p k e", k=2),
                                            bv_row[:, None, cols].to_broadcast([P, 2, UNIT]), ALU.add).then_inc(side_done, 1)
                    return
                dve.wait_ge(side_hi, hi_no(b, item) + 1)
                if kind == "T":
                    w, t = n // TT, slice(n % TT * P, (n % TT + 1) * P)
                    nc.vector.tensor_tensor(act_lo[w][:, :, t], blocks(bank), act_hi[w][:, :, t],
                                            ALU.subtract).then_inc(side_done, 1)
                if kind in "QK":
                    which = "QK".index(kind)
                    bias = (bq_neg, bk_col)[which][:, n % 4:n % 4 + 1]
                    nc.vector.scalar_tensor_tensor(out=qk_lo[which][:], in0=bank[:], scalar=bias, in1=qk_hi[which][:],
                                                   op0=ALU.add, op1=ALU.subtract).then_inc(side_done, 1)
                if kind == "R":
                    nc.vector.tensor_tensor(ctx_sb[:, n % 2, :], pv_bank[:], ctx_sb[:, n % 2, :],
                                            ALU.mult).then_inc(side_done, 1)

            def mask_and_min(b, c, i):
                _, _, q = where(c, i)
                k = i % TILES
                dve.wait_ge(s_mm, tile_no(b, c, i) + 1 + HEAD)
                dve.wait_ge(p_exp, tile_no(b, c, i) + 1)
                apart(dve)
                nc.vector.tensor_tensor_reduce(neg_s[:, i % SM_RING, :], s_bank[i % S_BANKS][:], mask_big[:, q, :], 1.0,
                                               3e38, ALU.add, ALU.min, negmax[:, k:k + 1]).then_inc(s_min, 1)

            def probs_out(b, c, i):
                _, j, q = where(c, i)
                dve.wait_ge(p_tr, tile_no(b, c, i) + 1 + P_RING)
                nc.vector.tensor_copy(pT[:, j, :, q * P:(q + 1) * P], blocks(pt_bank[i % 2])).then_inc(pt_out[0], 1)

            def reciprocals(b, c):
                g = b * GROUPS + c
                dve.wait_ge(p_exp, (g + 1) * TILES + SM_RING)
                dve.wait_ge(rden_ready, g + HEAD)
                nc.vector.reciprocal(rden[:], den[:, c % 2, :]).then_inc(rden_calc, 1)
                dve.wait_ge(rden_calc, g + 1)
                src = rden[:].rearrange("p (j q) -> p q j", j=GH)[:, :, :, None].to_broadcast([P, TT, GH, HD])
                nc.vector.tensor_copy(rden_rep[:], src).then_inc(rden_ready, 1)

            for kind, n in PROLOGUE:
                if kind == "K":
                    layer_stats(0)
                    split_w(1)
                    split_w(0)
                    dve.wait_ge(pool_chain, CHAIN)
                    for t in range(TT):
                        nc.vector.tensor_scalar(nat[0][:, t, :], nat[0][:, t, :], mv[:, t, 0:1], rstd[:, t:t + 1],
                                                ALU.subtract, ALU.mult).then_inc(xhat_done, 1)
                    split_w(2)
                if kind == "Q":
                    dve.wait_ge(consts, 1)
                side(None, kind, n)
                if kind == "Q":
                    dve.wait_ge(mask_ld, 16)
                    nc.vector.tensor_scalar(mask_big[:], mask_u8, MASKED, None, ALU.mult).then_inc(mask_done, 1)
                    dve.wait_ge(bv_ld, 16)
            dve.wait_ge(consts, 2)
            nc.vector.tensor_scalar(tgbo[:], tgbo[:], tg[:, 0:1], None, ALU.mult).then_inc(consts, 1)
            dve.wait_ge(mask_done, 1)
            for i in range(2):
                mask_and_min(0, 0, i)

            def tile_step(b, c, i):
                if not (is_last(b) and c == GROUPS - 1 and i + 2 >= TILES):
                    mask_and_min(b, c, i + 2)
                for kind, n in listed(LO_SIDE, b, c, i):
                    side(b, kind, n)
                if i % 2 == 0:
                    probs_out(b, c, i)

            def early_steps(b):
                for i in range(EARLY):
                    tile_step(b, 0, i)
                    if i == LO_STEP and not isinstance(b, int):
                        side(b - 1, "R", GROUPS - 1)

            def batch(b):
                for c in range(GROUPS):
                    for i in range(EARLY if c == 0 else 0, TILES):
                        tile_step(b, c, i)
                        if c == 1 and i == 3 and not is_last(b):
                            layer_stats(b + 1)
                        if is_last(b) and c == GROUPS - 1 and i in (2, 5, 8, 11):
                            n = (i - 2) // 3
                            dve.wait_ge(w2_hi_done, n + 1)
                            nc.vector.tensor_tensor(w2_lo[n][:], w2_raw[:, n % 2], w2_hi[n][:],
                                                    ALU.subtract).then_inc(w2_lo_done, 1)
                    reciprocals(b, c)
                    for kind, n in listed(LO_SIDE, b, c, END):
                        side(b, kind, n)
                if not is_last(b):
                    early_steps(b + 1)

            early_steps(0)
            with dve.Fori(0, B - 1) as b:
                batch(b)
            batch(B - 1)
            side(B - 1, "R", GROUPS - 1)

            def context_lo(b, h):
                dve.wait_ge(c2_hi, b * 2 + h + 1)
                nc.vector.tensor_tensor(c_lo[:], c_raw[:, h], c_hi[:], ALU.subtract).then_inc(c2_lo, 1)

            def residual1(b, h):
                u = b * 2 + h
                dve.wait_ge(xb_done, u + 1)
                if not (isinstance(b, int) and b == 0):
                    dve.wait_ge(o_done, u - 1 + HEAD)
                for m in range(UM):
                    dve.wait_ge(o_mm, u * UM + m + 1)
                    nc.vector.scalar_tensor_tensor(out=x1[:, h, m], in0=o_bank[m][:], scalar=tg[:, 0:1],
                                                   in1=x_in[:, h, m], op0=ALU.mult, op1=ALU.add).then_inc(x1_done, 1)
                dve.wait_ge(mv2_done, u * UM)
                dve.wait_ge(xh_done, u * UM)
                for m in range(UM):
                    dve.wait_ge(x1_done, u * UM + m + 1)
                    nc.vector.bn_stats(stats2[:, m, :], x1[:, h, m]).then_inc(bn2_done, 1)
                for m in range(UM):
                    dve.wait_ge(bn2_done, u * UM + m + 1)
                    apart(dve)
                    nc.vector.bn_aggr(mv2[:, m, :], stats2[:, m, :]).then_inc(mv2_done, 1)

            def normalise2(b, h):
                u = b * 2 + h
                dve.wait_ge(pool_chain2, (u + 1) * CHAIN)
                dve.wait_ge(t_mm, u * UM)
                for m in range(UM):
                    nc.vector.tensor_scalar(xh[:, m], x1[:, h, m], mv2[:, m, 0:1], rstd2[:, m:m + 1],
                                            ALU.subtract, ALU.mult).then_inc(xh_done, 1)

            def mixes(b, h):
                u = b * 2 + h
                dve.wait_ge(xT_done, (u + 1) * UM)
                if h == 1:
                    dve.wait_ge(carry_done, b + 1)
                dve.wait_ge(mix_done[1], u * CH)
                nc.vector.tensor_tensor(diff[:], xT[:, h, :, 1:1 + UNIT], xT[:, h, :, 0:UNIT],
                                        ALU.subtract).then_inc(diff_done, 1)
                dve.wait_ge(diff_done, u + 1)
                for n, mu in ((0, muk_col), (1, mur_col)):
                    dve.wait_ge(mixlo_done[n], u)
                    for a in range(CH):
                        nc.vector.scalar_tensor_tensor(out=mix[n][:, a], in0=diff[:, a], scalar=mu[:, a:a + 1],
                                                       in1=xT[:, h, a, 0:UNIT], op0=ALU.mult,
                                                       op1=ALU.add).then_inc(mix_done[n], 1)
                mixed_lo(b, h, 0)

            def mixed_lo(b, h, n):
                dve.wait_ge(mixhi_done[n], b * 2 + h + 1)
                nc.vector.tensor_tensor(mix_lo[n][:], mix[n][:], mix_hi[n][:], ALU.subtract).then_inc(mixlo_done[n], 1)

            def step2(b, h):
                u = b * 2 + h
                more = not (h and is_last(b))
                nb, nh = (b, 1) if h == 0 else (b + 1, 0)
                if more:
                    residual1(nb, nh)
                mixed_lo(b, h, 1)
                dve.wait_ge(kactlo_done, u + HEAD)
                for m in range(UM):
                    dve.wait_ge(relu_done, u * UM + m + 1)
                    nc.vector.scalar_tensor_tensor(out=kact[:, m], in0=k_bank[m][:], scalar=0.0, in1=relu[:, m],
                                                   op0=ALU.max, op1=ALU.mult).then_inc(kact_done, 1)
                dve.wait_ge(kacthi_done, u + 1)
                nc.vector.tensor_tensor(kact_lo[:].rearrange("p a t -> p (a t)"), kact[:].rearrange("p m d -> p (m d)"),
                                        kact_hi[:].rearrange("p a t -> p (a t)"), ALU.subtract).then_inc(kactlo_done, 1)
                if more:
                    normalise2(nb, nh)
                if not is_last(b):
                    context_lo(b + 1, h)
                if more:
                    mixes(nb, nh)
                dve.wait_ge(out_st[h], b * 16 + DMA_HEAD)
                for m in range(UM):
                    dve.wait_ge(v_mm, u * UM + m + 1)
                    dve.wait_ge(recept_done, u * UM + m + 1 + HEAD)
                    nc.vector.scalar_tensor_tensor(out=o_sb[:, h, m], in0=v_bank[m][:], scalar=tg[:, 1:2],
                                                   in1=recept[:, m], op0=ALU.mult, op1=ALU.mult).then_inc(y_done, 1)

            dve.wait_ge(c2_ld[0], 16)
            nc.vector.memset(xT[:, 0, :, 0:1], 0.0).then_inc(mask_done, 1)
            dve.wait_ge(mask_done, 2)
            context_lo(0, 0)
            dve.wait_ge(consts, 3)
            dve.wait_ge(o_mm, UM)
            context_lo(0, 1)
            residual1(0, 0)
            normalise2(0, 0)
            mixes(0, 0)
            with dve.Fori(0, B - 1) as b:
                step2(b, 0)
                step2(b, 1)
            step2(B - 1, 0)
            step2(B - 1, 1)

        @block.gpsimd
        def _(pool):
            for ring, length in ((side_done, SIDE_BANKS), (s_min, S_BANKS), (p_exp, SM_RING), (p_tr, P_RING)):
                pool.sem_inc(ring, length)
            for signal in (s_mm, *pt_out, rden_ready, kact_done, y_done, recept_done, kactlo_done, o_done):
                pool.sem_inc(signal, HEAD)
            for signal in (*ctx_st, *out_st):
                pool.sem_inc(signal, DMA_HEAD)
            def inverse_root(base, sem_, var, ve, y, t):
                n = [0]

                def link(ins):
                    n[0] += 1
                    ins.then_inc(sem_, 1)
                    pool.wait_ge(sem_, base + n[0])
                    apart(pool)

                link(nc.gpsimd.tensor_scalar(ve, var, EPS, None, ALU.add))
                link(nc.gpsimd.tensor_scalar(t.bitcast(I32), ve.bitcast(I32), -0.5, RSQRT_MAGIC, ALU.mult, ALU.add))
                link(nc.gpsimd.tensor_copy(y, t))
                for _ in range(NEWTON):
                    link(nc.gpsimd.tensor_tensor(t, y, y, ALU.mult))
                    link(nc.gpsimd.tensor_tensor(t, t, ve, ALU.mult))
                    link(nc.gpsimd.tensor_scalar(t, t, -0.5, 1.5, ALU.mult, ALU.add))
                    link(nc.gpsimd.tensor_tensor(y, y, t, ALU.mult))

            def normalise(b):
                pool.wait_ge(mv_done, (b + 1) * TT)
                apart(pool)
                inverse_root(b * CHAIN, pool_chain, mv[:, :, 1], var_eps[:], rstd[:], newton[:])
                if isinstance(b, int):
                    return
                for t in range(TT):
                    nc.gpsimd.tensor_scalar(nat[0][:, t, :], nat[0][:, t, :], mv[:, t, 0:1], rstd[:, t:t + 1],
                                            ALU.subtract, ALU.mult).then_inc(xhat_done, 1)

            normalise(0)
            with pool.Fori(0, B - 1) as b:
                normalise(b + 1)

            def add_bias(b, h):
                pool.wait_ge(x2_ld[h], b * 16 + 16)
                nc.gpsimd.tensor_tensor(x_in[:, h], x_in[:, h], tgbo[:, None, :].to_broadcast([P, UM, D]),
                                        ALU.add).then_inc(xb_done, 1)

            def inverse_root2(b, h):
                u = b * 2 + h
                pool.wait_ge(mv2_done, (u + 1) * UM)
                apart(pool)
                inverse_root(u * CHAIN, pool_chain2, mv2[:, :, 1], var_eps2[:], rstd2[:], newton2[:])

            def step2(b, h):
                u = b * 2 + h
                if not (h and is_last(b)):
                    inverse_root2(*((b, 1) if h == 0 else (b + 1, 0)))
                if not is_last(b):
                    add_bias(b + 1, h)
                pool.wait_ge(y_done, (u + 1) * UM + HEAD)
                nc.gpsimd.tensor_tensor(o_sb[:, h], o_sb[:, h], x1[:, h], ALU.add).then_inc(o_done, 1)

            pool.wait_ge(consts, 3)
            add_bias(0, 0)
            add_bias(0, 1)
            inverse_root2(0, 0)
            with pool.Fori(0, B - 1) as b:
                step2(b, 0)
                step2(b, 1)
            step2(B - 1, 0)
            step2(B - 1, 1)


def kernel(x, ctx_1024, mask_SxS2_bk1, g_xattn, g_ffn, L0_xattn_q_w, L0_xattn_q_b, L0_xattn_k_w, L0_xattn_k_b,
           L0_xattn_v_w, L0_xattn_v_b, L0_xattn_o_w, L0_xattn_o_b, L0_ffn_W_r, L0_ffn_W_k, L0_ffn_W_v, L0_ffn_mu_r,
           L0_ffn_mu_k):
    import numpy as np
    import concourse.bacc as bacc
    from concourse.bass_utils import run_bass_kernel_spmd

    def turned(w):
        return np.ascontiguousarray(np.asarray(w).T)

    def columns(v):
        return np.ascontiguousarray(np.asarray(v).reshape(CH, P).T)

    def row(v):
        return np.asarray(v).reshape(1, -1)

    arrays = {
        "x": np.asarray(x).reshape(B * S, D),
        "ctx": np.asarray(ctx_1024).reshape(B * S, D),
        "mask": np.asarray(mask_SxS2_bk1),
        "g_xattn": row(g_xattn), "g_ffn": row(g_ffn),
        "wqT": turned(L0_xattn_q_w), "bq": columns(L0_xattn_q_b),
        "wkT": turned(L0_xattn_k_w), "bk": columns(L0_xattn_k_b),
        "wvT": turned(L0_xattn_v_w), "bv": row(L0_xattn_v_b),
        "woT": turned(L0_xattn_o_w), "bo": row(L0_xattn_o_b),
        "wrT": turned(L0_ffn_W_r), "wkkT": turned(L0_ffn_W_k), "wvvT": turned(L0_ffn_W_v),
        "mur": columns(L0_ffn_mu_r), "muk": columns(L0_ffn_mu_k),
        "ident_d": np.eye(P, dtype=np.float32),
    }
    nc = bacc.Bacc("TRN2", target_bir_lowering=False, num_devices=1)
    args = [nc.dram_tensor(name, a.shape, mybir.dt.from_np(a.dtype), kind="ExternalInput").ap()
            for name, a in arrays.items()]
    out = nc.dram_tensor("out", (B * S, D), F32, kind="ExternalOutput").ap()
    ctx_dram = nc.dram_tensor("ctx_dram", (B * D, S), F32, kind="Internal").ap()
    build(nc, *args, out, ctx_dram)
    result = run_bass_kernel_spmd(nc, [arrays], core_ids=[0])
    return result.results[0]["out"].reshape(B, S, D)
```

```python
from contextlib import ExitStack

import concourse.bass as bass
from concourse import mybir

F32 = mybir.dt.float32
F32R = mybir.dt.float32r
BF16 = mybir.dt.bfloat16
U8 = mybir.dt.uint8
I32 = mybir.dt.int32
ALU = mybir.AluOpType
ACT = mybir.ActivationFunctionType

P = 128
B, S, D = 8, 512, 512
NH, HD = 16, 32
CH = D // P
TT = S // P
GH = P // HD
GROUPS = NH // GH
TILES = GH * TT
EPS = 1e-5
SCALE = 1.0 / float(HD) ** 0.5
MASKED = 2.0 ** 100
RSQRT_MAGIC = float(0x5F3759DF)
NEWTON = 3

TERMS = 3
END = TILES + 1


def parts(kind, n, *steps):
    return {step: [(kind, n, part, len(steps))] for part, step in enumerate(steps)}


T_STEPS = (7, 8, 9, 11, 12, 14, 15, 16)
PE_SIDE = [
    parts("Q", 1, 0, 1, 2) | parts("K", 1, 3, 4, 6) | parts("V", 2, 8, 9, 10, 11, 12, 13, 14, 16),
    parts("Q", 2, 0, 1, 2) | parts("K", 2, 3, 4, 6) | parts("V", 3, 8, 9, 10, 11, 12, 13, 14, 16),
    parts("Q", 3, 0, 1, 2) | parts("K", 3, 3, 4, 6) | {step: [("T", n, 0, 1)] for n, step in enumerate(T_STEPS)},
    parts("Q", 4, 0, 1, 2) | parts("K", 4, 3, 4, 6) | parts("V", 0, 7, 8, 9, 10) | parts("V", 1, 11, 12, 13, 14, 15, 16),
]


def out_side(lag, r_step):
    table = [{} for _ in range(GROUPS)]
    for c in range(GROUPS):
        for step, items in PE_SIDE[c].items():
            kind, n, part, of = items[0]
            if part == of - 1:
                at = step + 1 + (lag if kind != "V" else 0)
                table[c].setdefault(at if at < TILES else END, []).append((kind, n))
        table[c][r_step] = [("R", (c - 1) % GROUPS)] + table[c].get(r_step, [])
    return table


HI_STEP, LO_STEP = 1, 2
HI_SIDE, LO_SIDE = out_side(0, HI_STEP), out_side(1, LO_STEP)
EARLY = LO_STEP + 1
PROLOGUE = [("T", n) for n in (4, 5, 6, 7)] + [("K", 0)] + [("T", n) for n in range(4)] + [("Q", 0), ("V", 0), ("V", 1)]
NEXT_BATCH = [("T", n) for n in range(8)] + [("Q", 4), ("K", 4), ("V", 0), ("V", 1)]
ORDER = [item for c in range(GROUPS) for item in
         [i[:2] for step in range(END) for i in PE_SIDE[c].get(step, []) if i[2] == 0] + [("R", c)]]
ORDER_LAST = [item for item in ORDER if item not in NEXT_BATCH]
SIDE_BANKS = 3
SIDE_PER_BATCH = len(ORDER)
HI_PER_BATCH, HI_PROLOGUE = (len([i for i in items if i[0] != "V"]) for items in (ORDER, PROLOGUE))
assert SIDE_PER_BATCH % SIDE_BANKS == 0

SM_RING, P_RING, S_BANKS = 4, 4, 2
HEAD = 1
DMA_HEAD = 16
STACK_DMAS = 6
UNIT = 256
UM = UNIT // P
SPLIT_W2 = ((2, 17), (3, 3), (3, 10), (3, 17))
FIRST_CONTEXT = (3, 1)
FIRST_O = (3, 4, 5, 6, 7, 8)
FIRST_RESIDUAL = (3, 9)
FIRST_NORM = (3, 15)


def build(nc, x, ctx_in, mask, g_xattn, g_ffn, wq, bq, wk, bk, wv, bv, wo, bo, wr, wkk, wvv, mur, muk, ident_d, out, ctx_dram):
    keep = ExitStack()
    stage1 = ExitStack()
    stage2 = ExitStack()

    def sem(name):
        return keep.enter_context(nc.semaphore(name))

    def sb(stack, name, shape, dt=F32):
        return stack.enter_context(nc.sbuf_tensor(name, shape, dt))

    with keep:
        banks = [keep.enter_context(nc.psum_tensor(f"bank{i}", [P, 512], F32)) for i in range(8)]
        ident = sb(keep, "ident", [P, P])
        gates = sb(keep, "gates", [P, 2])
        tg = sb(keep, "tg", [P, 2])
        bq_col = sb(keep, "bq_col", [P, CH])
        bq_neg = sb(keep, "bq_neg", [P, CH])
        bk_col = sb(keep, "bk_col", [P, CH])
        mur_col = sb(keep, "mur_col", [P, CH])
        muk_col = sb(keep, "muk_col", [P, CH])
        bv_row = sb(keep, "bv_row", [P, D])
        tgbo = sb(keep, "tgbo", [P, D])
        stats2 = sb(keep, "stats2", [P, UM, 6])
        mv2 = sb(keep, "mv2", [P, UM, 2])
        var_eps2 = sb(keep, "var_eps2", [P, UM])
        newton2 = sb(keep, "newton2", [P, UM])
        rstd2 = sb(keep, "rstd2", [P, UM])

        w1_hi = [sb(stage1, f"w{n}_hi", [P, CH, D], F32R) for n in "qkv"]
        w1_lo = [sb(stage1, f"w{n}_lo", [P, CH, D], F32R) for n in "qkv"]
        act_hi = [sb(stage1, f"{n}T_hi", [P, CH, S], F32R) for n in ("x", "c")]
        act_lo = [sb(stage1, f"{n}T_lo", [P, CH, S], F32R) for n in ("x", "c")]
        nat = [sb(stage1, f"{n}_nat", [P, TT, D]) for n in ("x", "c")]
        qk_hi = [sb(stage1, f"{n}_hi", [P, S], F32R) for n in "qk"]
        qk_lo = [sb(stage1, f"{n}_lo", [P, S], F32R) for n in "qk"]
        stack = [[sb(stage1, f"{n}_stack{s}", [3 * HD, GH, S], F32R) for n in "qk"] for s in range(2)]
        v_sb = sb(stage1, "v_sb", [P, TT, D])
        pT = sb(stage1, "pT", [P, GH, TT, S])
        neg_s = sb(stage1, "neg_s", [P, SM_RING, S])
        probs = sb(stage1, "probs", [P, P_RING, S])
        mask_big = sb(stage1, "mask_big", [P, TT, S], BF16)
        negmax = sb(stage1, "negmax", [P, TILES])
        den = sb(stage1, "den", [P, 2, TILES])
        rden = sb(stage1, "rden", [P, TILES])
        rden_rep = sb(stage1, "rden_rep", [P, TT, GH, HD])
        ctx_sb = sb(stage1, "ctx_sb", [P, 2, S])
        stats = sb(stage1, "stats", [P, TT, 6])
        mv = sb(stage1, "mv", [P, TT, 2])
        var_eps = sb(stage1, "var_eps", [P, TT])
        newton = sb(stage1, "newton", [P, TT])
        rstd = sb(stage1, "rstd", [P, TT])
        mask_u8 = probs[:].rearrange("p r k -> p (r k)").bitcast(U8)[:, 0:TT * S].rearrange("p (t k) -> p t k", t=TT)
        stage1.close()

        w2_hi = [sb(stage2, f"w2{n}_hi", [P, CH, D], F32R) for n in "okrv"]
        w2_lo = [sb(stage2, f"w2{n}_lo", [P, CH, D], F32R) for n in "okrv"]
        w2_raw = sb(stage2, "w2_raw", [P, 2, CH, D])
        c_raw = sb(stage2, "c_raw", [P, 2, CH, UNIT])
        x_in = sb(stage2, "x_in", [P, 2, UM, D])
        c_hi = sb(stage2, "c_hi", [P, CH, UNIT], F32R)
        c_lo = sb(stage2, "c_lo", [P, CH, UNIT], F32R)
        x1 = sb(stage2, "x1", [P, 2, UM, D])
        xh = sb(stage2, "xh", [P, UM, D])
        diff = sb(stage2, "diff", [P, CH, UNIT])
        xT = sb(stage2, "xT", [P, 2, CH, 1 + UNIT])
        mix = [sb(stage2, f"mix_{n}", [P, CH, UNIT]) for n in "kr"]
        mix_hi = [sb(stage2, f"mix_{n}_hi", [P, CH, UNIT], F32R) for n in "kr"]
        mix_lo = [sb(stage2, f"mix_{n}_lo", [P, CH, UNIT], F32R) for n in "kr"]
        relu = sb(stage2, "relu", [P, UM, D])
        kact = sb(stage2, "kact", [P, UM, D])
        kact_hi = sb(stage2, "kact_hi", [P, CH, UNIT], F32R)
        kact_lo = sb(stage2, "kact_lo", [P, CH, UNIT], F32R)
        recept = sb(stage2, "recept", [P, UM, D])
        o_sb = sb(stage2, "o_sb", [P, 2, UM, D])
        stage2.close()

        s_bank, pt_bank, pv_bank, side_bank = banks[0:2], banks[2:4], banks[4], banks[5:8]
        k_bank, r_bank, v_bank, o_bank = banks[0:2], banks[2:4], (banks[4], banks[7]), banks[5:7]

        small_ld, bias_ld, bv_ld = sem("small_ld"), sem("bias_ld"), sem("bv_ld")
        unused = sem("unused")
        ident_ld = sem("ident_ld")
        mask_ld = sem("mask_ld")
        w_ld = [sem(f"w_ld{n}") for n in range(3)]
        consts = sem("consts")
        mask_done = sem("mask_done")
        w_hi_done, w_lo_done = sem("w_hi_done"), sem("w_lo_done")
        x_ld, c_ld = sem("x_ld"), sem("c_ld")
        bn_done, mv_done, pool_chain, xhat_done = sem("bn_done"), sem("mv_done"), sem("pool_chain"), sem("xhat_done")
        side_mm, side_hi, side_done = sem("side_mm"), sem("side_hi"), sem("side_done")
        stacked = [sem(f"stacked_head{j}") for j in range(GH)]
        s_mm, s_min, p_exp, p_tr = sem("s_mm"), sem("s_min"), sem("p_exp"), sem("p_tr")
        pt_out = [sem("pt_out_dve"), sem("pt_out_act")]
        rden_calc, rden_ready = sem("rden_calc"), sem("rden_ready")
        ctx_st = [sem("ctx_st0"), sem("ctx_st1")]
        w2_ld = [sem("w2_ld0"), sem("w2_ld1")]
        w2_hi_done, w2_lo_done = sem("w2_hi_done"), [sem(f"w2_lo_done{n}") for n in range(4)]
        c2_ld, x2_ld = [sem("c2_ld0"), sem("c2_ld1")], [sem("x2_ld0"), sem("x2_ld1")]
        c2_hi, c2_lo, xb_done = sem("c2_hi"), sem("c2_lo"), sem("xb_done")
        o_mm, x1_done, bn2_done, mv2_done = sem("o_mm"), sem("x1_done"), sem("bn2_done"), sem("mv2_done")
        pool_chain2, xh_done, t_mm, xT_done, carry_done = (
            sem("pool_chain2"), sem("xh_done"), sem("t_mm"), sem("xT_done"), sem("carry_done"))
        diff_done, mix_done, mixhi_done, mixlo_done = sem("diff_done"), [sem("mixk"), sem("mixr")], [
            sem("mixk_hi"), sem("mixr_hi")], [sem("mixk_lo"), sem("mixr_lo")]
        k_mm, r_mm, v_mm = sem("k_mm"), sem("r_mm"), sem("v_mm")
        relu_done, kact_done, kacthi_done, kactlo_done, recept_done = (
            sem("relu_done"), sem("kact_done"), sem("kacthi_done"), sem("kactlo_done"), sem("recept_done"))
        y_done, o_done = sem("y_done"), sem("o_done")
        out_st = [sem("out_st0"), sem("out_st1")]

        def side_no(b, item):
            if b is None:
                return PROLOGUE.index(item)
            order = ORDER_LAST if isinstance(b, int) and b == B - 1 else ORDER
            return b * SIDE_PER_BATCH + len(PROLOGUE) + order.index(item)

        def side_bank_of(b, item):
            if b is None:
                return side_bank[PROLOGUE.index(item) % SIDE_BANKS]
            order = ORDER_LAST if isinstance(b, int) and b == B - 1 else ORDER
            return side_bank[(len(PROLOGUE) + order.index(item)) % SIDE_BANKS]

        def hi_no(b, item):
            if b is None:
                return PROLOGUE.index(item)
            order = [i for i in (ORDER_LAST if isinstance(b, int) and b == B - 1 else ORDER) if i[0] != "V"]
            return b * HI_PER_BATCH + HI_PROLOGUE + order.index(item)

        def done(number):
            return number + 1 + SIDE_BANKS

        def listed(table, b, c, step):
            return [i for i in table[c].get(step, []) if not (is_last(b) and i[:2] in NEXT_BATCH)
                    and not (c == 0 and i[:2] == ("R", GROUPS - 1))]

        def previous_r(b, c):
            return done(side_no(b, ("R", c - 1))) if c else b * SIDE_PER_BATCH + len(PROLOGUE) + SIDE_BANKS

        def is_last(b):
            return isinstance(b, int) and b == B - 1

        def tile_no(b, c, i):
            return b * (GROUPS * TILES) + (c * TILES + i)

        def where(c, i):
            c, i = c + i // TILES, i % TILES
            return c % 2, i // TT, i % TT

        def blocks(bank):
            return bank[:].rearrange("p (a t) -> p a t", a=TT)

        def apart(engine):
            engine.sem_inc(unused, 1)

        CHAIN = 3 + 4 * NEWTON

        block = keep.enter_context(nc.Block())

        @block.sync
        def _(sp):
            def load_rows(which, rows, b):
                sp.dma_start(nat[which][:], rows[bass.ds(b * S, S), :].rearrange("(t p) c -> p t c", p=P)).then_inc(
                    (x_ld, c_ld)[which], 16)

            def load_w(n, w):
                sp.dma_start(pT[:, n, :, :], w.rearrange("(a p) e -> p a e", p=P)).then_inc(w_ld[n], 16)

            sp.dma_start(ident[:], ident_d).then_inc(ident_ld, 16)
            load_rows(1, ctx_in, 0)
            load_rows(0, x, 0)
            load_w(1, wk)
            for t, a in ((bq_col, bq), (bk_col, bk)):
                sp.dma_start(t[:], a).then_inc(bias_ld, 16)
            load_w(0, wq)
            load_w(2, wv)
            sp.dma_start(mask_u8, mask.rearrange("(t p) k -> p t k", p=P)).then_inc(mask_ld, 16)
            sp.dma_start(bv_row[:], bv.to_broadcast([P, D])).then_inc(bv_ld, 16)
            for t, a in ((mur_col, mur), (muk_col, muk)):
                sp.dma_start(t[:], a).then_inc(small_ld, 16)
            sp.dma_start(gates[:, 0:1], g_xattn.to_broadcast([P, 1])).then_inc(small_ld, 16)
            sp.dma_start(gates[:, 1:2], g_ffn.to_broadcast([P, 1])).then_inc(small_ld, 16)
            sp.dma_start(tgbo[:], bo.to_broadcast([P, D])).then_inc(small_ld, 16)

            def stack_rows(kind, n, bands, source, heads):
                dst = stack[n % 2]["QK".index(kind)]
                for j in heads:
                    for band in bands:
                        sp.dma_start(dst[HD * band:HD * (band + 1), j, :].bitcast(F32),
                                     source[HD * j:HD * (j + 1), :].bitcast(F32)).then_inc(stacked[j], 16)

            def stack_q_hi(b, n, heads):
                sp.wait_ge(side_hi, hi_no(b, ("Q", n)) + 1)
                apart(sp)
                stack_rows("Q", n, (0, 1), qk_hi[0], heads)

            def stack_q_lo(b, n, heads):
                sp.wait_ge(side_done, done(side_no(b, ("Q", n))))
                apart(sp)
                stack_rows("Q", n, (2,), qk_lo[0], heads)

            def stack_k(b, n, heads):
                sp.wait_ge(side_done, done(side_no(b, ("K", n))))
                apart(sp)
                for j in heads:
                    stack_rows("K", n, (0, 2), qk_hi[1], (j,))
                    stack_rows("K", n, (1,), qk_lo[1], (j,))

            def stack_group(b, n):
                stack_q_hi(b, n, (0, 1, 2))
                stack_q_lo(b, n, (0, 1, 2))
                stack_k(b, n, (0,))
                stack_q_hi(b, n, (3,))
                stack_q_lo(b, n, (3,))
                stack_k(b, n, (1, 2, 3))

            stack_k(None, 0, range(GH))
            for j in range(GH):
                stack_q_hi(None, 0, (j,))
                stack_q_lo(None, 0, (j,))

            def load_unit(b, h):
                sp.dma_start(c_raw[:, h], ctx_dram[bass.ds(b * D, D), :].rearrange("(a p) t -> p a t", p=P)[
                    :, :, h * UNIT:(h + 1) * UNIT]).then_inc(c2_ld[h], 16)
                sp.dma_start(x_in[:, h], x[bass.ds(b * S + h * UNIT, UNIT), :].rearrange(
                    "(m p) c -> p m c", p=P)).then_inc(x2_ld[h], 16)

            W2 = (wo, wkk, wr, wvv)

            def load_w2(n):
                if n >= 2:
                    sp.wait_ge(w2_lo_done[n - 2], 1)
                sp.dma_start(w2_raw[:, n % 2], W2[n].rearrange("(a p) e -> p a e", p=P)).then_inc(w2_ld[n % 2], 16)

            def batch(b):
                for c in range(GROUPS):
                    for step in range(END + 1):
                        for kind, n in listed(LO_SIDE, b, c, step) + [("R", c)] * (c == GROUPS - 1 and step == END):
                            if kind == "Q":
                                sp.wait_ge(s_mm, tile_no(b, c, 0) + HEAD)
                                apart(sp)
                                if is_last(b) and n == GROUPS - 1:
                                    sp.wait_ge(side_mm, side_no(b, ("Q", n)) + 1)
                                    apart(sp)
                                    load_w2(0)
                                stack_group(b, n)
                                if is_last(b) and n == GROUPS - 1:
                                    load_unit(0, 0)
                                    load_w2(1)
                                    load_unit(0, 1)
                                    load_w2(2)
                                    load_w2(3)
                            if kind == "R":
                                sp.wait_ge(side_done, done(side_no(b, (kind, n))))
                                apart(sp)
                                sp.dma_start(ctx_dram[bass.ds(b * D + n * P, P), :], ctx_sb[:, n % 2, :]).then_inc(
                                    ctx_st[n % 2], 16)
                    if c == 0 and not is_last(b):
                        sp.wait_ge(side_mm, b * SIDE_PER_BATCH + len(PROLOGUE))
                        apart(sp)
                        load_rows(0, x, b + 1)
                        load_rows(1, ctx_in, b + 1)
            with sp.Fori(0, B - 1) as b:
                batch(b)
            batch(B - 1)

            for s in range(2):
                sp.wait_ge(ctx_st[s], 16 * 2 * B + DMA_HEAD)

            def step2(b, h):
                if not is_last(b):
                    sp.wait_ge(c2_lo, b * 2 + h + 1)
                    apart(sp)
                    sp.wait_ge(x1_done, (b * 2 + h + 1) * UM)
                    apart(sp)
                    load_unit(b + 1, h)
                sp.wait_ge(o_done, b * 2 + h + 1 + HEAD)
                apart(sp)
                sp.dma_start(out[bass.ds(b * S + h * UNIT, UNIT), :].rearrange("(m p) c -> p m c", p=P),
                             o_sb[:, h]).then_inc(out_st[h], 16)

            with sp.Fori(0, B - 1) as b:
                step2(b, 0)
                step2(b, 1)
            step2(B - 1, 0)
            step2(B - 1, 1)
            for s in range(2):
                sp.wait_ge(out_st[s], 16 * B + DMA_HEAD)

        @block.tensor
        def _(pe):
            def one_term(part, dst, w_hi, w_lo, r_hi, r_lo, lhs, rhs):
                left, right = ((w_hi, r_lo), (w_lo, r_hi), (w_hi, r_hi))[part]
                for a in range(CH):
                    mm = nc.tensor.matmul(dst, lhs(left, a), rhs(right, a), start=(part == 0 and a == 0),
                                          stop=(part == TERMS - 1 and a == CH - 1))
                return mm

            def three_terms(*operands):
                for part in range(TERMS):
                    mm = one_term(part, *operands)
                return mm

            def side(b, kind, n, part, of):
                item = (kind, n)
                bank = side_bank_of(b, item)
                if part == 0:
                    pe.wait_ge(side_done, side_no(b, item) + 1)
                if kind == "T":
                    of_batch = 0 if b is None else b + 1
                    if n < TT:
                        pe.wait_ge(xhat_done, of_batch * TT + n + 1)
                    else:
                        pe.wait_ge(c_ld, of_batch * 16 + 16)
                    rows = nat[n // TT][:, n % TT, :]
                    for a in range(CH):
                        mm = nc.tensor.transpose(bank[:, a * P:(a + 1) * P], rows[:, a * P:(a + 1) * P], ident[:])
                if kind in "QK":
                    which = "QK".index(kind)
                    if n in (0, 4) and part == 0:
                        pe.wait_ge(side_done, done(side_no(b, ("T", TT * which + TT - 1))))
                    cols = slice((n % 4) * P, (n % 4 + 1) * P)
                    w_hi, w_lo, r_hi, r_lo = w1_hi[which], w1_lo[which], act_hi[which], act_lo[which]
                    share = TERMS * CH // of
                    for at in range(part * share, (part + 1) * share):
                        left, right = ((w_hi, r_lo), (w_lo, r_hi), (w_hi, r_hi))[at // CH]
                        mm = nc.tensor.matmul(bank[:], left[:, at % CH, cols], right[:, at % CH, :],
                                              start=(at == 0), stop=(at == TERMS * CH - 1))
                if kind == "V":
                    share = 2 * TERMS * CH // of
                    for at in range(part * share, (part + 1) * share):
                        k, term, a = at // (TERMS * CH), at // CH % TERMS, at % CH
                        keys = 2 * (n % 2) + k
                        left, right = ((act_hi[1], w1_lo[2]), (act_lo[1], w1_hi[2]), (act_hi[1], w1_hi[2]))[term]
                        mm = nc.tensor.matmul(bank[:, k * UNIT:(k + 1) * UNIT], left[:, a, keys * P:(keys + 1) * P],
                                              right[:, a, n // 2 * UNIT:(n // 2 + 1) * UNIT],
                                              start=(term == 0 and a == 0), stop=(term == TERMS - 1 and a == CH - 1))
                if kind == "R":
                    pe.wait_ge(rden_ready, b * GROUPS + n + 1 + HEAD)
                    for q in range(TT):
                        mm = nc.tensor.transpose(bank[:, q * P:(q + 1) * P],
                                                 rden_rep[:, q].rearrange("p j d -> p (j d)"), ident[:])
                if part == of - 1:
                    mm.then_inc(side_mm, 1)

            def scores(b, c, i):
                slot, j, q = where(c, i)
                if i % TT == 0:
                    pe.wait_ge(stacked[j], (b * GROUPS + c + i // TILES + 1) * STACK_DMAS * 16)
                pe.wait_ge(s_min, tile_no(b, c, i) + 1)
                nc.tensor.matmul(s_bank[i % S_BANKS][:], stack[slot][0][:, j, q * P:(q + 1) * P],
                                 stack[slot][1][:, j, :], start=True, stop=True).then_inc(s_mm, 1)

            def transpose_probs(b, c, i):
                pe.wait_ge(p_exp, tile_no(b, c, i) + 1 + SM_RING)
                pe.wait_ge(pt_out[i % 2], b * (GROUPS * TILES // 2) + (c * TILES + i) // 2 + HEAD)
                for a in range(TT):
                    mm = nc.tensor.transpose(pt_bank[i % 2][:, a * P:(a + 1) * P],
                                             probs[:, i % P_RING, a * P:(a + 1) * P], ident[:])
                mm.then_inc(p_tr, 1)

            def context(b, c):
                for s in range(2):
                    pe.wait_ge(pt_out[s], (b * GROUPS + c + 1) * (TILES // 2) + HEAD)
                pe.wait_ge(side_done, previous_r(b, c))
                for a in range(TT):
                    for j in range(GH):
                        head = c * GH + j
                        nc.tensor.matmul(pv_bank[j * HD:(j + 1) * HD, :], v_sb[:, a, head * HD:(head + 1) * HD],
                                         pT[:, j, a, :], start=(a == 0), stop=(a == TT - 1))

            pe.wait_ge(ident_ld, 16)
            for kind, n in PROLOGUE:
                if kind != "T":
                    pe.wait_ge(w_lo_done, 1 + "KQV".index(kind))
                side(None, kind, n, 0, 1)
            for i in range(3):
                scores(0, 0, i)

            def batch(b):
                for c in range(GROUPS):
                    for i in range(TILES):
                        if i and not (is_last(b) and c == GROUPS - 1 and i + 2 >= TILES):
                            scores(b, c, i + 2)
                        for item in listed(PE_SIDE, b, c, i):
                            side(b, *item)
                        if is_last(b) and c == GROUPS - 1 and i in FIRST_O:
                            first_o_proj(FIRST_O.index(i))
                        transpose_probs(b, c, i)
                    for item in listed(PE_SIDE, b, c, TILES):
                        side(b, *item)
                    if is_last(b) and c == GROUPS - 1:
                        transposes(0, 0)
                    else:
                        scores(b, c, TILES + 2)
                    context(b, c)
                    side(b, "R", c, 0, 1)

            def first_o_proj(at):
                m, part = at // TERMS, at % TERMS
                if at == 0:
                    pe.wait_ge(w2_lo_done[0], 1)
                    pe.wait_ge(c2_lo, 1)
                    pe.wait_ge(side_done, done(side_no(B - 1, ("R", GROUPS - 2))))
                mm = one_term(part, o_bank[m][:], c_hi, c_lo, w2_hi[0], w2_lo[0],
                              lambda w, a: w[:, a, m * P:(m + 1) * P], lambda r, a: r[:, a, :])
                if part == TERMS - 1:
                    mm.then_inc(o_mm, 1)

            def transposes(b, h):
                u = b * 2 + h
                if isinstance(b, int) and b + h == 0:
                    pe.wait_ge(s_min, B * GROUPS * TILES + S_BANKS)
                else:
                    pe.wait_ge(kact_done, u * UM + HEAD)
                for m in range(UM):
                    pe.wait_ge(xh_done, u * UM + m + 1)
                    for a in range(CH):
                        mm = nc.tensor.transpose(k_bank[m][:, a * P:(a + 1) * P], xh[:, m, a * P:(a + 1) * P], ident[:])
                    mm.then_inc(t_mm, 1)

            with pe.Fori(0, B - 1) as b:
                batch(b)
            batch(B - 1)

            def o_proj(b, h):
                u = b * 2 + h
                pe.wait_ge(c2_lo, u + 1)
                pe.wait_ge(x1_done, u * UM)
                for m in range(UM):
                    three_terms(o_bank[m][:], c_hi, c_lo, w2_hi[0], w2_lo[0],
                                lambda w, a: w[:, a, m * P:(m + 1) * P], lambda r, a: r[:, a, :]).then_inc(o_mm, 1)

            def k_proj(b, h):
                pe.wait_ge(w2_lo_done[1], 1)
                pe.wait_ge(mixlo_done[0], b * 2 + h + 1)
                for m in range(UM):
                    for half in range(2):
                        n = 2 * m + half
                        mm = three_terms(k_bank[m][:, half * UNIT:(half + 1) * UNIT], w2_hi[1], w2_lo[1],
                                         mix_hi[0], mix_lo[0], lambda w, a: w[:, a, n * P:(n + 1) * P],
                                         lambda r, a: r[:, a, :])
                    mm.then_inc(k_mm, 1)

            def r_proj(b, h):
                u = b * 2 + h
                pe.wait_ge(w2_lo_done[2], 1)
                pe.wait_ge(mixlo_done[1], u + 1)
                pe.wait_ge(recept_done, u * UM + HEAD)
                for m in range(UM):
                    three_terms(r_bank[m][:], mix_hi[1], mix_lo[1], w2_hi[2], w2_lo[2],
                                lambda w, a: w[:, a, m * P:(m + 1) * P], lambda r, a: r[:, a, :]).then_inc(r_mm, 1)

            def v_proj(b, h):
                u = b * 2 + h
                pe.wait_ge(w2_lo_done[3], 1)
                pe.wait_ge(kactlo_done, u + 1 + HEAD)
                pe.wait_ge(y_done, u * UM + HEAD)
                for m in range(UM):
                    three_terms(v_bank[m][:], kact_hi, kact_lo, w2_hi[3], w2_lo[3],
                                lambda w, a: w[:, a, m * P:(m + 1) * P], lambda r, a: r[:, a, :]).then_inc(v_mm, 1)

            o_proj(0, 1)

            def step2(b, h):
                k_proj(b, h)
                r_proj(b, h)
                if h == 0:
                    transposes(b, 1)
                elif not is_last(b):
                    transposes(b + 1, 0)
                v_proj(b, h)
                if not is_last(b):
                    o_proj(b + 1, h)

            with pe.Fori(0, B - 1) as b:
                step2(b, 0)
                step2(b, 1)
            step2(B - 1, 0)
            step2(B - 1, 1)

        @block.scalar
        def _(act):
            def split_w(n):
                act.wait_ge(w_ld[n], 16)
                nc.scalar.mul(w1_hi[n][:], pT[:, n], -SCALE if n == 0 else 1.0).then_inc(w_hi_done, 1)

            def side(b, kind, n):
                item = (kind, n)
                bank = side_bank_of(b, item)
                if kind == "V":
                    return
                if kind == "Q" and n:
                    for copied in stacked:
                        act.wait_ge(copied, (b * GROUPS + n) * STACK_DMAS * 16)
                if kind == "R":
                    act.wait_ge(ctx_st[n % 2], (b * 2 + n // 2) * 16 + DMA_HEAD)
                act.wait_ge(side_mm, side_no(b, item) + 1)
                if kind == "T":
                    t = n % TT
                    nc.scalar.copy(act_hi[n // TT][:, :, t * P:(t + 1) * P], blocks(bank)).then_inc(side_hi, 1)
                if kind in "QK":
                    which = "QK".index(kind)
                    bias = (bq_neg, bk_col)[which][:, n % 4:n % 4 + 1]
                    nc.scalar.activation(qk_hi[which][:], bank[:], ACT.Identity, bias=bias).then_inc(side_hi, 1)
                if kind == "R":
                    nc.scalar.copy(ctx_sb[:, n % 2, :], bank[:]).then_inc(side_hi, 1)

            def exp(b, c, i):
                if i == TILES:
                    act.wait_ge(rden_ready, b * GROUPS + c + HEAD)
                act.wait_ge(s_min, tile_no(b, c, i) + 1 + S_BANKS)
                act.wait_ge(p_tr, tile_no(b, c, i) + 1)
                g = (c + i // TILES) % 2
                k = i % TILES
                nc.scalar.activation(probs[:, i % P_RING, :], neg_s[:, i % SM_RING, :], ACT.Exp,
                                     bias=negmax[:, k:k + 1], scale=-1.0,
                                     accum_out=den[:, g, k:k + 1]).then_inc(p_exp, 1)

            def probs_out(b, c, i):
                _, j, q = where(c, i)
                act.wait_ge(p_tr, tile_no(b, c, i) + 1 + P_RING)
                nc.scalar.copy(pT[:, j, :, q * P:(q + 1) * P], blocks(pt_bank[i % 2])).then_inc(pt_out[1], 1)

            for kind, n in PROLOGUE:
                if kind == "K":
                    split_w(1)
                    act.wait_ge(bias_ld, 16 * 2)
                    nc.scalar.mul(bq_neg[:], bq_col[:], -SCALE).then_inc(consts, 1)
                    split_w(0)
                    split_w(2)
                if kind == "Q":
                    act.wait_ge(consts, 1)
                side(None, kind, n)
                if kind == "Q":
                    act.wait_ge(small_ld, 16 * 5)
                    nc.scalar.activation(tg[:], gates[:], ACT.Tanh).then_inc(consts, 1)
            exp(0, 0, 0)

            def tile_step(b, c, i):
                for kind, n in listed(HI_SIDE, b, c, i):
                    side(b, kind, n)
                if not (is_last(b) and c == GROUPS - 1 and i + 1 >= TILES):
                    exp(b, c, i + 1)
                if i % 2:
                    probs_out(b, c, i)

            def early_steps(b):
                for i in range(EARLY):
                    tile_step(b, 0, i)
                    if i == HI_STEP and not isinstance(b, int):
                        side(b - 1, "R", GROUPS - 1)

            def batch(b):
                for c in range(GROUPS):
                    for i in range(EARLY if c == 0 else 0, TILES):
                        tile_step(b, c, i)
                        if is_last(b) and (c, i) in SPLIT_W2:
                            split_w2(SPLIT_W2.index((c, i)))
                        if is_last(b) and (c, i) == FIRST_CONTEXT:
                            context_hi(0, 0)
                    for kind, n in listed(HI_SIDE, b, c, END):
                        side(b, kind, n)
                    if is_last(b) and (c, END) in SPLIT_W2:
                        split_w2(SPLIT_W2.index((c, END)))
                    if is_last(b) and c == GROUPS - 1:
                        context_hi(0, 1)
                if not is_last(b):
                    early_steps(b + 1)

            def split_w2(n):
                act.wait_ge(w2_ld[n % 2], 16 * (n // 2 + 1))
                nc.scalar.copy(w2_hi[n][:], w2_raw[:, n % 2]).then_inc(w2_hi_done, 1)

            def context_hi(b, h):
                act.wait_ge(c2_ld[h], b * 16 + 16)
                if isinstance(b, int) and b + h == 0:
                    for copied in stacked:
                        act.wait_ge(copied, B * GROUPS * STACK_DMAS * 16)
                act.wait_ge(o_mm, (b * 2 + h) * UM)
                nc.scalar.copy(c_hi[:], c_raw[:, h]).then_inc(c2_hi, 1)

            early_steps(0)
            with act.Fori(0, B - 1) as b:
                batch(b)
            batch(B - 1)
            def xT_out(b, h):
                u = b * 2 + h
                if h == 1:
                    act.wait_ge(xT_done, u * UM)
                    nc.scalar.copy(xT[:, 1, :, 0:1], xT[:, 0, :, UNIT:UNIT + 1]).then_inc(carry_done, 1)
                for m in range(UM):
                    act.wait_ge(t_mm, u * UM + m + 1)
                    nc.scalar.copy(xT[:, h, :, 1 + m * P:1 + (m + 1) * P], blocks(k_bank[m])).then_inc(xT_done, 1)

            xT_out(0, 0)
            side(B - 1, "R", GROUPS - 1)

            def mixed_hi(b, h, n):
                act.wait_ge(mix_done[n], (b * 2 + h + 1) * CH)
                nc.scalar.copy(mix_hi[n][:], mix[n][:]).then_inc(mixhi_done[n], 1)

            def step2(b, h):
                u = b * 2 + h
                for m in range(UM):
                    act.wait_ge(kact_done, u * UM + HEAD)
                    act.wait_ge(k_mm, u * UM + m + 1)
                    nc.scalar.activation(relu[:, m], k_bank[m][:], ACT.Relu).then_inc(relu_done, 1)
                act.wait_ge(kact_done, (u + 1) * UM + HEAD)
                nc.scalar.copy(kact_hi[:].rearrange("p a t -> p (a t)"),
                               kact[:].rearrange("p m d -> p (m d)")).then_inc(kacthi_done, 1)
                if not is_last(b):
                    context_hi(b + 1, h)
                act.wait_ge(y_done, u * UM + HEAD)
                for m in range(UM):
                    act.wait_ge(r_mm, u * UM + m + 1)
                    nc.scalar.activation(recept[:, m], r_bank[m][:], ACT.Sigmoid).then_inc(recept_done, 1)
                if not (h and is_last(b)):
                    nb, nh = (b, 1) if h == 0 else (b + 1, 0)
                    xT_out(nb, nh)
                    mixed_hi(nb, nh, 0)
                    mixed_hi(nb, nh, 1)

            mixed_hi(0, 0, 0)
            mixed_hi(0, 0, 1)
            with act.Fori(0, B - 1) as b:
                step2(b, 0)
                step2(b, 1)
            step2(B - 1, 0)
            step2(B - 1, 1)

        @block.vector
        def _(dve):
            def split_w(n):
                dve.wait_ge(w_hi_done, 1 + (1, 0, 2).index(n))
                nc.vector.scalar_tensor_tensor(out=w1_lo[n][:], in0=pT[:, n], scalar=-SCALE if n == 0 else 1.0,
                                               in1=w1_hi[n][:], op0=ALU.mult, op1=ALU.subtract).then_inc(w_lo_done, 1)

            def row_stats(b, t):
                if t == 0:
                    dve.wait_ge(x_ld, b * 16 + 16)
                    dve.wait_ge(mv_done, b * TT)
                nc.vector.bn_stats(stats[:, t, :], nat[0][:, t, :]).then_inc(bn_done, 1)

            def mean_and_variance(b):
                dve.wait_ge(xhat_done, b * TT)
                for t in range(TT):
                    dve.wait_ge(bn_done, b * TT + t + 1)
                    apart(dve)
                    nc.vector.bn_aggr(mv[:, t, :], stats[:, t, :]).then_inc(mv_done, 1)

            def side(b, kind, n):
                item = (kind, n)
                bank = side_bank_of(b, item)
                if kind == "V":
                    dve.wait_ge(side_mm, side_no(b, item) + 1)
                    cols = slice(n // 2 * UNIT, (n // 2 + 1) * UNIT)
                    nc.vector.tensor_tensor(v_sb[:, 2 * (n % 2):2 * (n % 2) + 2, cols],
                                            bank[:].rearrange("p (k e) -> p k e", k=2),
                                            bv_row[:, None, cols].to_broadcast([P, 2, UNIT]), ALU.add).then_inc(side_done, 1)
                    return
                dve.wait_ge(side_hi, hi_no(b, item) + 1)
                if kind == "T":
                    w, t = n // TT, slice(n % TT * P, (n % TT + 1) * P)
                    nc.vector.tensor_tensor(act_lo[w][:, :, t], blocks(bank), act_hi[w][:, :, t],
                                            ALU.subtract).then_inc(side_done, 1)
                if kind in "QK":
                    which = "QK".index(kind)
                    bias = (bq_neg, bk_col)[which][:, n % 4:n % 4 + 1]
                    nc.vector.scalar_tensor_tensor(out=qk_lo[which][:], in0=bank[:], scalar=bias, in1=qk_hi[which][:],
                                                   op0=ALU.add, op1=ALU.subtract).then_inc(side_done, 1)
                if kind == "R":
                    nc.vector.tensor_tensor(ctx_sb[:, n % 2, :], pv_bank[:], ctx_sb[:, n % 2, :],
                                            ALU.mult).then_inc(side_done, 1)

            def mask_and_min(b, c, i):
                _, _, q = where(c, i)
                k = i % TILES
                dve.wait_ge(s_mm, tile_no(b, c, i) + 1 + HEAD)
                dve.wait_ge(p_exp, tile_no(b, c, i) + 1)
                apart(dve)
                nc.vector.tensor_tensor_reduce(neg_s[:, i % SM_RING, :], s_bank[i % S_BANKS][:], mask_big[:, q, :], 1.0,
                                               3e38, ALU.add, ALU.min, negmax[:, k:k + 1]).then_inc(s_min, 1)

            def probs_out(b, c, i):
                _, j, q = where(c, i)
                dve.wait_ge(p_tr, tile_no(b, c, i) + 1 + P_RING)
                nc.vector.tensor_copy(pT[:, j, :, q * P:(q + 1) * P], blocks(pt_bank[i % 2])).then_inc(pt_out[0], 1)

            def reciprocals(b, c):
                g = b * GROUPS + c
                dve.wait_ge(p_exp, (g + 1) * TILES + SM_RING)
                dve.wait_ge(rden_ready, g + HEAD)
                nc.vector.reciprocal(rden[:], den[:, c % 2, :]).then_inc(rden_calc, 1)
                dve.wait_ge(rden_calc, g + 1)
                src = rden[:].rearrange("p (j q) -> p q j", j=GH)[:, :, :, None].to_broadcast([P, TT, GH, HD])
                nc.vector.tensor_copy(rden_rep[:], src).then_inc(rden_ready, 1)

            for kind, n in PROLOGUE:
                if kind == "K":
                    for t in range(TT):
                        row_stats(0, t)
                    mean_and_variance(0)
                    split_w(1)
                    split_w(0)
                    dve.wait_ge(pool_chain, CHAIN)
                    for t in range(TT):
                        nc.vector.tensor_scalar(nat[0][:, t, :], nat[0][:, t, :], mv[:, t, 0:1], rstd[:, t:t + 1],
                                                ALU.subtract, ALU.mult).then_inc(xhat_done, 1)
                    split_w(2)
                if kind == "Q":
                    dve.wait_ge(consts, 1)
                side(None, kind, n)
                if kind == "Q":
                    dve.wait_ge(mask_ld, 16)
                    nc.vector.tensor_scalar(mask_big[:], mask_u8, MASKED, None, ALU.mult).then_inc(mask_done, 1)
                    dve.wait_ge(bv_ld, 16)
            dve.wait_ge(consts, 2)
            nc.vector.tensor_scalar(tgbo[:], tgbo[:], tg[:, 0:1], None, ALU.mult).then_inc(consts, 1)
            dve.wait_ge(mask_done, 1)
            for i in range(2):
                mask_and_min(0, 0, i)

            def tile_step(b, c, i):
                for kind, n in listed(LO_SIDE, b, c, i):
                    side(b, kind, n)
                if not (is_last(b) and c == GROUPS - 1 and i + 2 >= TILES):
                    mask_and_min(b, c, i + 2)
                if i % 2 == 0:
                    probs_out(b, c, i)

            def early_steps(b):
                for i in range(EARLY):
                    tile_step(b, 0, i)
                    if i == LO_STEP and not isinstance(b, int):
                        side(b - 1, "R", GROUPS - 1)

            def batch(b):
                for c in range(GROUPS):
                    for i in range(EARLY if c == 0 else 0, TILES):
                        tile_step(b, c, i)
                        if c == 1 and 3 <= i < 3 + TT and not is_last(b):
                            row_stats(b + 1, i - 3)
                        if c == 1 and i == 3 + TT and not is_last(b):
                            mean_and_variance(b + 1)
                        if is_last(b) and (c, i) == FIRST_CONTEXT:
                            context_lo(0, 0)
                        if is_last(b) and (c, i) == FIRST_RESIDUAL:
                            residual1(0, 0)
                        if is_last(b) and (c, i) == FIRST_NORM:
                            normalise2(0, 0)
                    reciprocals(b, c)
                    if is_last(b) and c == GROUPS - 2:
                        dve.wait_ge(w2_hi_done, 1)
                        nc.vector.tensor_tensor(w2_lo[0][:], w2_raw[:, 0], w2_hi[0][:], ALU.subtract).then_inc(w2_lo_done[0], 1)
                    if is_last(b) and c == GROUPS - 1:
                        context_lo(0, 1)
                    for kind, n in listed(LO_SIDE, b, c, END):
                        side(b, kind, n)
                if not is_last(b):
                    early_steps(b + 1)

            def context_lo(b, h):
                dve.wait_ge(c2_hi, b * 2 + h + 1)
                nc.vector.tensor_tensor(c_lo[:], c_raw[:, h], c_hi[:], ALU.subtract).then_inc(c2_lo, 1)

            def residual1(b, h):
                u = b * 2 + h
                dve.wait_ge(xb_done, u + 1)
                if isinstance(b, int) and b + h == 0:
                    dve.wait_ge(consts, 3)
                if not (isinstance(b, int) and b == 0):
                    dve.wait_ge(o_done, u - 1 + HEAD)
                for m in range(UM):
                    dve.wait_ge(o_mm, u * UM + m + 1)
                    nc.vector.scalar_tensor_tensor(out=x1[:, h, m], in0=o_bank[m][:], scalar=tg[:, 0:1],
                                                   in1=x_in[:, h, m], op0=ALU.mult, op1=ALU.add).then_inc(x1_done, 1)
                dve.wait_ge(mv2_done, u * UM)
                dve.wait_ge(xh_done, u * UM)
                for m in range(UM):
                    dve.wait_ge(x1_done, u * UM + m + 1)
                    nc.vector.bn_stats(stats2[:, m, :], x1[:, h, m]).then_inc(bn2_done, 1)
                for m in range(UM):
                    dve.wait_ge(bn2_done, u * UM + m + 1)
                    apart(dve)
                    nc.vector.bn_aggr(mv2[:, m, :], stats2[:, m, :]).then_inc(mv2_done, 1)

            def normalise2(b, h):
                u = b * 2 + h
                dve.wait_ge(pool_chain2, (u + 1) * CHAIN)
                dve.wait_ge(t_mm, u * UM)
                for m in range(UM):
                    nc.vector.tensor_scalar(xh[:, m], x1[:, h, m], mv2[:, m, 0:1], rstd2[:, m:m + 1],
                                            ALU.subtract, ALU.mult).then_inc(xh_done, 1)

            early_steps(0)
            with dve.Fori(0, B - 1) as b:
                batch(b)
            batch(B - 1)
            def difference(b, h):
                u = b * 2 + h
                dve.wait_ge(xT_done, (u + 1) * UM)
                if h == 1:
                    dve.wait_ge(carry_done, b + 1)
                dve.wait_ge(mix_done[1], u * CH)
                nc.vector.tensor_tensor(diff[:], xT[:, h, :, 1:1 + UNIT], xT[:, h, :, 0:UNIT],
                                        ALU.subtract).then_inc(diff_done, 1)
                dve.wait_ge(diff_done, u + 1)

            def mixed(b, h, n):
                dve.wait_ge(mixlo_done[n], b * 2 + h)
                for a in range(CH):
                    nc.vector.scalar_tensor_tensor(out=mix[n][:, a], in0=diff[:, a], scalar=(muk_col, mur_col)[n][:, a:a + 1],
                                                   in1=xT[:, h, a, 0:UNIT], op0=ALU.mult,
                                                   op1=ALU.add).then_inc(mix_done[n], 1)

            def mixed_lo(b, h, n):
                dve.wait_ge(mixhi_done[n], b * 2 + h + 1)
                nc.vector.tensor_tensor(mix_lo[n][:], mix[n][:], mix_hi[n][:], ALU.subtract).then_inc(mixlo_done[n], 1)

            def step2(b, h):
                u = b * 2 + h
                more = not (h and is_last(b))
                nb, nh = (b, 1) if h == 0 else (b + 1, 0)
                if more:
                    residual1(nb, nh)
                mixed_lo(b, h, 1)
                dve.wait_ge(kactlo_done, u + HEAD)
                for m in range(UM):
                    dve.wait_ge(relu_done, u * UM + m + 1)
                    nc.vector.scalar_tensor_tensor(out=kact[:, m], in0=k_bank[m][:], scalar=0.0, in1=relu[:, m],
                                                   op0=ALU.max, op1=ALU.mult).then_inc(kact_done, 1)
                dve.wait_ge(kacthi_done, u + 1)
                nc.vector.tensor_tensor(kact_lo[:].rearrange("p a t -> p (a t)"), kact[:].rearrange("p m d -> p (m d)"),
                                        kact_hi[:].rearrange("p a t -> p (a t)"), ALU.subtract).then_inc(kactlo_done, 1)
                if more:
                    normalise2(nb, nh)
                if not is_last(b):
                    context_lo(b + 1, h)
                if more:
                    difference(nb, nh)
                    mixed(nb, nh, 0)
                    mixed(nb, nh, 1)
                    mixed_lo(nb, nh, 0)
                dve.wait_ge(out_st[h], b * 16 + DMA_HEAD)
                for m in range(UM):
                    dve.wait_ge(v_mm, u * UM + m + 1)
                    dve.wait_ge(recept_done, u * UM + m + 1 + HEAD)
                    nc.vector.scalar_tensor_tensor(out=o_sb[:, h, m], in0=v_bank[m][:], scalar=tg[:, 1:2],
                                                   in1=recept[:, m], op0=ALU.mult, op1=ALU.mult).then_inc(y_done, 1)

            nc.vector.memset(xT[:, 0, :, 0:1], 0.0).then_inc(mask_done, 1)
            dve.wait_ge(mask_done, 2)
            difference(0, 0)
            mixed(0, 0, 0)
            side(B - 1, "R", GROUPS - 1)
            mixed(0, 0, 1)
            mixed_lo(0, 0, 0)
            with dve.Fori(0, B - 1) as b:
                step2(b, 0)
                step2(b, 1)
            step2(B - 1, 0)
            step2(B - 1, 1)

        @block.gpsimd
        def _(pool):
            for ring, length in ((side_done, SIDE_BANKS), (s_min, S_BANKS), (p_exp, SM_RING), (p_tr, P_RING)):
                pool.sem_inc(ring, length)
            for signal in (s_mm, *pt_out, rden_ready, kact_done, y_done, recept_done, kactlo_done, o_done):
                pool.sem_inc(signal, HEAD)
            for signal in (*ctx_st, *out_st):
                pool.sem_inc(signal, DMA_HEAD)
            def inverse_root(base, sem_, var, ve, y, t):
                n = [0]

                def link(ins):
                    n[0] += 1
                    ins.then_inc(sem_, 1)
                    pool.wait_ge(sem_, base + n[0])
                    apart(pool)

                link(nc.gpsimd.tensor_scalar(ve, var, EPS, None, ALU.add))
                link(nc.gpsimd.tensor_scalar(t.bitcast(I32), ve.bitcast(I32), -0.5, RSQRT_MAGIC, ALU.mult, ALU.add))
                link(nc.gpsimd.tensor_copy(y, t))
                for _ in range(NEWTON):
                    link(nc.gpsimd.tensor_tensor(t, y, y, ALU.mult))
                    link(nc.gpsimd.tensor_tensor(t, t, ve, ALU.mult))
                    link(nc.gpsimd.tensor_scalar(t, t, -0.5, 1.5, ALU.mult, ALU.add))
                    link(nc.gpsimd.tensor_tensor(y, y, t, ALU.mult))

            def normalise(b):
                pool.wait_ge(mv_done, (b + 1) * TT)
                apart(pool)
                inverse_root(b * CHAIN, pool_chain, mv[:, :, 1], var_eps[:], rstd[:], newton[:])
                if isinstance(b, int):
                    return
                for t in range(TT):
                    nc.gpsimd.tensor_scalar(nat[0][:, t, :], nat[0][:, t, :], mv[:, t, 0:1], rstd[:, t:t + 1],
                                            ALU.subtract, ALU.mult).then_inc(xhat_done, 1)

            normalise(0)
            with pool.Fori(0, B - 1) as b:
                normalise(b + 1)

            def add_bias(b, h):
                pool.wait_ge(x2_ld[h], b * 16 + 16)
                nc.gpsimd.tensor_tensor(x_in[:, h], x_in[:, h], tgbo[:, None, :].to_broadcast([P, UM, D]),
                                        ALU.add).then_inc(xb_done, 1)

            def inverse_root2(b, h):
                u = b * 2 + h
                pool.wait_ge(mv2_done, (u + 1) * UM)
                apart(pool)
                inverse_root(u * CHAIN, pool_chain2, mv2[:, :, 1], var_eps2[:], rstd2[:], newton2[:])

            def step2(b, h):
                u = b * 2 + h
                if not (h and is_last(b)):
                    inverse_root2(*((b, 1) if h == 0 else (b + 1, 0)))
                if not is_last(b):
                    add_bias(b + 1, h)
                pool.wait_ge(y_done, (u + 1) * UM + HEAD)
                nc.gpsimd.tensor_tensor(o_sb[:, h], o_sb[:, h], x1[:, h], ALU.add).then_inc(o_done, 1)

            def split_w2(n):
                pool.wait_ge(w2_hi_done, n + 1)
                nc.gpsimd.tensor_tensor(w2_lo[n][:], w2_raw[:, n % 2], w2_hi[n][:], ALU.subtract).then_inc(w2_lo_done[n], 1)

            pool.wait_ge(consts, 3)
            add_bias(0, 0)
            split_w2(1)
            inverse_root2(0, 0)
            split_w2(2)
            add_bias(0, 1)
            split_w2(3)
            with pool.Fori(0, B - 1) as b:
                step2(b, 0)
                step2(b, 1)
            step2(B - 1, 0)
            step2(B - 1, 1)


def kernel(x, ctx_1024, mask_SxS2_bk1, g_xattn, g_ffn, L0_xattn_q_w, L0_xattn_q_b, L0_xattn_k_w, L0_xattn_k_b,
           L0_xattn_v_w, L0_xattn_v_b, L0_xattn_o_w, L0_xattn_o_b, L0_ffn_W_r, L0_ffn_W_k, L0_ffn_W_v, L0_ffn_mu_r,
           L0_ffn_mu_k):
    import numpy as np
    import concourse.bacc as bacc
    from concourse.bass_utils import run_bass_kernel_spmd

    def turned(w):
        return np.ascontiguousarray(np.asarray(w).T)

    def columns(v):
        return np.ascontiguousarray(np.asarray(v).reshape(CH, P).T)

    def row(v):
        return np.asarray(v).reshape(1, -1)

    arrays = {
        "x": np.asarray(x).reshape(B * S, D),
        "ctx": np.asarray(ctx_1024).reshape(B * S, D),
        "mask": np.asarray(mask_SxS2_bk1),
        "g_xattn": row(g_xattn), "g_ffn": row(g_ffn),
        "wqT": turned(L0_xattn_q_w), "bq": columns(L0_xattn_q_b),
        "wkT": turned(L0_xattn_k_w), "bk": columns(L0_xattn_k_b),
        "wvT": turned(L0_xattn_v_w), "bv": row(L0_xattn_v_b),
        "woT": turned(L0_xattn_o_w), "bo": row(L0_xattn_o_b),
        "wrT": turned(L0_ffn_W_r), "wkkT": turned(L0_ffn_W_k), "wvvT": turned(L0_ffn_W_v),
        "mur": columns(L0_ffn_mu_r), "muk": columns(L0_ffn_mu_k),
        "ident_d": np.eye(P, dtype=np.float32),
    }
    nc = bacc.Bacc("TRN2", target_bir_lowering=False, num_devices=1)
    args = [nc.dram_tensor(name, a.shape, mybir.dt.from_np(a.dtype), kind="ExternalInput").ap()
            for name, a in arrays.items()]
    out = nc.dram_tensor("out", (B * S, D), F32, kind="ExternalOutput").ap()
    ctx_dram = nc.dram_tensor("ctx_dram", (B * D, S), F32, kind="Internal").ap()
    build(nc, *args, out, ctx_dram)
    result = run_bass_kernel_spmd(nc, [arrays], core_ids=[0])
    return result.results[0]["out"].reshape(B, S, D)
```

```python
from contextlib import ExitStack

import concourse.bass as bass
from concourse import mybir

F32 = mybir.dt.float32
F32R = mybir.dt.float32r
BF16 = mybir.dt.bfloat16
U8 = mybir.dt.uint8
I32 = mybir.dt.int32
ALU = mybir.AluOpType
ACT = mybir.ActivationFunctionType

P = 128
B, S, D = 8, 512, 512
NH, HD = 16, 32
CH = D // P
TT = S // P
GH = P // HD
GROUPS = NH // GH
TILES = GH * TT
EPS = 1e-5
SCALE = 1.0 / float(HD) ** 0.5
MASKED = 2.0 ** 100
RSQRT_MAGIC = float(0x5F3759DF)
NEWTON = 3

TERMS = 3
END = TILES + 1


def parts(kind, n, *steps):
    return {step: [(kind, n, part, len(steps))] for part, step in enumerate(steps)}


PE_SIDE = [
    parts("K", 1, 0, 1, 3, 4) | parts("V", 2, 6, 7, 8, 9, 10, 11) | parts("Q", 2, 12, 13, 14, 16),
    parts("K", 2, 0, 1, 3, 4) | parts("V", 3, 6, 7, 8, 9, 10, 11) | parts("Q", 3, 12, 13, 14, 16),
    {step: [("T", n, 0, 1)] for n, step in enumerate((0, 1, 3, 4))} | parts("K", 3, 5, 6, 7)
    | parts("Q", 4, 9, 10, 12, 13, 14, 16),
    parts("K", 4, 0, 1, 2) | parts("V", 0, 3, 4, 5, 6) | parts("V", 1, 7, 8, 9, 10)
    | parts("Q", 5, 11, 12, 13, 14, 15, 16),
]
PE_SIDE[2][TILES] += [("C", n, 0, 1) for n in range(CH)]


def out_side(lag, r_step):
    table = [{} for _ in range(GROUPS)]
    for c in range(GROUPS):
        for step, items in PE_SIDE[c].items():
            for kind, n, part, of in items:
                if part == of - 1:
                    at = step + 1 + (lag if kind != "V" else 0)
                    table[c].setdefault(at if at < TILES else END, []).append((kind, n))
        table[c][r_step] = [("R", (c - 1) % GROUPS)] + table[c].get(r_step, [])
    return table


STATS_STEPS = (8, 10, 12, 14)
HI_STEP, LO_STEP = 1, 2
HI_SIDE, LO_SIDE = out_side(0, HI_STEP), out_side(1, LO_STEP)
EARLY = LO_STEP + 1
C_ITEMS, T_ITEMS = [("C", n) for n in range(CH)], [("T", n) for n in range(TT)]
PROLOGUE = C_ITEMS + [("K", 0)] + T_ITEMS + [("Q", 0), ("V", 0), ("V", 1), ("Q", 1)]
NEXT_BATCH = C_ITEMS + T_ITEMS + [("Q", 4), ("K", 4), ("V", 0), ("V", 1), ("Q", 5)]
ORDER = [item for c in range(GROUPS) for item in
         [i[:2] for step in range(END) for i in PE_SIDE[c].get(step, []) if i[2] == 0] + [("R", c)]]
ORDER_LAST = [item for item in ORDER if item not in NEXT_BATCH]
SIDE_BANKS = 3
SIDE_PER_BATCH = len(ORDER)
MM_PER_BATCH, MM_PROLOGUE = (len([i for i in items if i[0] != "C"]) for items in (ORDER, PROLOGUE))
HI_PER_BATCH, HI_PROLOGUE = (len([i for i in items if i[0] != "V"]) for items in (ORDER, PROLOGUE))
assert SIDE_PER_BATCH % SIDE_BANKS == 0

SM_RING, P_RING, S_BANKS = 4, 4, 2
HEAD = 1
DMA_HEAD = 16
STACK_DMAS = 3
UNIT = 256
UM = UNIT // P
SPLIT_W2 = ((2, END), (3, 3), (3, 10), (3, END))
FIRST_CONTEXT = (3, 1)
FIRST_O = (3, 4, 5, 6, 7, 8)
FIRST_RESIDUAL = (3, 9)
FIRST_NORM = (3, 15)


def build(nc, x, ctxT, mask, g_xattn, g_ffn, wq, bq, wk, bk, wv, bv, wo, bo, wr, wkk, wvv, mur, muk, ident_d, out,
          ctx_dram):
    keep = ExitStack()
    stage1 = ExitStack()
    stage2 = ExitStack()

    def sem(name):
        return keep.enter_context(nc.semaphore(name))

    def sb(stack, name, shape, dt=F32):
        return stack.enter_context(nc.sbuf_tensor(name, shape, dt))

    with keep:
        banks = [keep.enter_context(nc.psum_tensor(f"bank{i}", [P, 512], F32)) for i in range(8)]
        ident = sb(keep, "ident", [P, P])
        gates = sb(keep, "gates", [P, 2])
        tg = sb(keep, "tg", [P, 2])
        bq_col = sb(keep, "bq_col", [P, CH])
        bq_neg = sb(keep, "bq_neg", [P, CH])
        bk_col = sb(keep, "bk_col", [P, CH])
        mur_col = sb(keep, "mur_col", [P, CH])
        muk_col = sb(keep, "muk_col", [P, CH])
        bv_row = sb(keep, "bv_row", [P, D])
        tgbo = sb(keep, "tgbo", [P, D])
        stats2 = sb(keep, "stats2", [P, UM, 6])
        mv2 = sb(keep, "mv2", [P, UM, 2])
        var_eps2 = sb(keep, "var_eps2", [P, UM])
        newton2 = sb(keep, "newton2", [P, UM])
        rstd2 = sb(keep, "rstd2", [P, UM])

        w1_hi = [sb(stage1, f"w{n}_hi", [P, CH, D], F32R) for n in "qkv"]
        w1_lo = [sb(stage1, f"w{n}_lo", [P, CH, D], F32R) for n in "qkv"]
        act_hi = [sb(stage1, f"{n}T_hi", [P, CH, S], F32R) for n in ("x", "c")]
        act_lo = [sb(stage1, f"{n}T_lo", [P, CH, S], F32R) for n in ("x", "c")]
        x_rows = sb(stage1, "x_rows", [P, TT, D])
        cT_raw = sb(stage1, "cT_raw", [P, CH, S])
        qk_hi = [sb(stage1, f"{n}_hi", [P, S], F32R) for n in "qk"]
        qk_lo = [sb(stage1, f"{n}_lo", [P, S], F32R) for n in "qk"]
        stack = [[sb(stage1, f"{n}_stack{s}", [3 * HD, GH, S], F32R) for n in "qk"] for s in range(2)]
        v_sb = sb(stage1, "v_sb", [P, TT, D])
        pT = sb(stage1, "pT", [P, GH, TT, S])
        neg_s = sb(stage1, "neg_s", [P, SM_RING, S])
        probs = sb(stage1, "probs", [P, P_RING, S])
        mask_big = sb(stage1, "mask_big", [P, TT, S], BF16)
        negmax = sb(stage1, "negmax", [P, TILES])
        den = sb(stage1, "den", [P, 2, TILES])
        rden = sb(stage1, "rden", [P, TILES])
        rden_rep = sb(stage1, "rden_rep", [P, TT, GH, HD])
        ctx_sb = sb(stage1, "ctx_sb", [P, 2, S])
        stats = sb(stage1, "stats", [P, TT, 6])
        mv = sb(stage1, "mv", [P, TT, 2])
        var_eps = sb(stage1, "var_eps", [P, TT])
        newton = sb(stage1, "newton", [P, TT])
        rstd = sb(stage1, "rstd", [P, TT])
        mask_u8 = probs[:].rearrange("p r k -> p (r k)").bitcast(U8)[:, 0:TT * S].rearrange("p (t k) -> p t k", t=TT)
        stage1.close()

        w2_hi = [sb(stage2, f"w2{n}_hi", [P, CH, D], F32R) for n in "okrv"]
        w2_lo = [sb(stage2, f"w2{n}_lo", [P, CH, D], F32R) for n in "okrv"]
        w2_raw = sb(stage2, "w2_raw", [P, 2, CH, D])
        c_raw = sb(stage2, "c_raw", [P, 2, CH, UNIT])
        x_in = sb(stage2, "x_in", [P, 2, UM, D])
        c_hi = sb(stage2, "c_hi", [P, CH, UNIT], F32R)
        c_lo = sb(stage2, "c_lo", [P, CH, UNIT], F32R)
        x1 = sb(stage2, "x1", [P, 2, UM, D])
        xh = sb(stage2, "xh", [P, UM, D])
        diff = sb(stage2, "diff", [P, CH, UNIT])
        xT = sb(stage2, "xT", [P, 2, CH, 1 + UNIT])
        mix = [sb(stage2, f"mix_{n}", [P, CH, UNIT]) for n in "kr"]
        mix_hi = [sb(stage2, f"mix_{n}_hi", [P, CH, UNIT], F32R) for n in "kr"]
        mix_lo = [sb(stage2, f"mix_{n}_lo", [P, CH, UNIT], F32R) for n in "kr"]
        relu = sb(stage2, "relu", [P, UM, D])
        kact = sb(stage2, "kact", [P, UM, D])
        kact_hi = sb(stage2, "kact_hi", [P, CH, UNIT], F32R)
        kact_lo = sb(stage2, "kact_lo", [P, CH, UNIT], F32R)
        recept = sb(stage2, "recept", [P, UM, D])
        o_sb = sb(stage2, "o_sb", [P, 2, UM, D])
        stage2.close()

        s_bank, pt_bank, pv_bank, side_bank = banks[0:2], banks[2:4], banks[4], banks[5:8]
        k_bank, r_bank, v_bank, o_bank = banks[0:2], banks[2:4], (banks[4], banks[7]), banks[5:7]

        small_ld, bias_ld, bv_ld = sem("small_ld"), sem("bias_ld"), sem("bv_ld")
        unused = sem("unused")
        ident_ld = sem("ident_ld")
        mask_ld = sem("mask_ld")
        w_ld = [sem(f"w_ld{n}") for n in range(3)]
        consts = sem("consts")
        mask_done = sem("mask_done")
        w_hi_done, w_lo_done = sem("w_hi_done"), sem("w_lo_done")
        x_ld, c_ld = sem("x_ld"), sem("c_ld")
        bn_done, mv_done, pool_chain, xhat_done = sem("bn_done"), sem("mv_done"), sem("pool_chain"), sem("xhat_done")
        side_mm, side_hi, side_done = sem("side_mm"), sem("side_hi"), sem("side_done")
        stacked = [[sem(f"{n}_stacked_head{j}") for j in range(GH)] for n in "qk"]
        s_mm, s_min, p_exp, p_tr = sem("s_mm"), sem("s_min"), sem("p_exp"), sem("p_tr")
        pt_out = [sem("pt_out_dve"), sem("pt_out_act")]
        rden_calc, rden_ready = sem("rden_calc"), sem("rden_ready")
        ctx_st = [sem("ctx_st0"), sem("ctx_st1")]
        w2_ld = [sem("w2_ld0"), sem("w2_ld1")]
        w2_hi_done, w2_lo_done = sem("w2_hi_done"), [sem(f"w2_lo_done{n}") for n in range(4)]
        c2_ld, x2_ld = [sem("c2_ld0"), sem("c2_ld1")], [sem("x2_ld0"), sem("x2_ld1")]
        c2_hi, c2_lo, xb_done = sem("c2_hi"), sem("c2_lo"), sem("xb_done")
        o_mm, x1_done, bn2_done, mv2_done = sem("o_mm"), sem("x1_done"), sem("bn2_done"), sem("mv2_done")
        pool_chain2, xh_done, t_mm, xT_done, carry_done = (
            sem("pool_chain2"), sem("xh_done"), sem("t_mm"), sem("xT_done"), sem("carry_done"))
        diff_done, mix_done, mixhi_done, mixlo_done = sem("diff_done"), [sem("mixk"), sem("mixr")], [
            sem("mixk_hi"), sem("mixr_hi")], [sem("mixk_lo"), sem("mixr_lo")]
        k_mm, r_mm, v_mm = sem("k_mm"), sem("r_mm"), sem("v_mm")
        relu_done, kact_done, kacthi_done, kactlo_done, recept_done = (
            sem("relu_done"), sem("kact_done"), sem("kacthi_done"), sem("kactlo_done"), sem("recept_done"))
        y_done, o_done = sem("y_done"), sem("o_done")
        out_st = [sem("out_st0"), sem("out_st1")]

        def side_no(b, item):
            if b is None:
                return PROLOGUE.index(item)
            order = ORDER_LAST if isinstance(b, int) and b == B - 1 else ORDER
            return b * SIDE_PER_BATCH + len(PROLOGUE) + order.index(item)

        def side_bank_of(b, item):
            if b is None:
                return side_bank[PROLOGUE.index(item) % SIDE_BANKS]
            order = ORDER_LAST if isinstance(b, int) and b == B - 1 else ORDER
            return side_bank[(len(PROLOGUE) + order.index(item)) % SIDE_BANKS]

        def mm_no(b, item):
            order = PROLOGUE if b is None else ORDER_LAST if isinstance(b, int) and b == B - 1 else ORDER
            at = [i for i in order if i[0] != "C"].index(item)
            return at if b is None else b * MM_PER_BATCH + MM_PROLOGUE + at

        def hi_no(b, item):
            if b is None:
                return [i for i in PROLOGUE if i[0] != "V"].index(item)
            order = [i for i in (ORDER_LAST if isinstance(b, int) and b == B - 1 else ORDER) if i[0] != "V"]
            return b * HI_PER_BATCH + HI_PROLOGUE + order.index(item)

        def done(number):
            return number + 1 + SIDE_BANKS

        def listed(table, b, c, step):
            return [i for i in table[c].get(step, []) if not (is_last(b) and i[:2] in NEXT_BATCH)
                    and not (c == 0 and i[:2] == ("R", GROUPS - 1))]

        def previous_r(b, c):
            return done(side_no(b, ("R", c - 1))) if c else b * SIDE_PER_BATCH + len(PROLOGUE) + SIDE_BANKS

        def is_last(b):
            return isinstance(b, int) and b == B - 1

        def tile_no(b, c, i):
            return b * (GROUPS * TILES) + (c * TILES + i)

        def where(c, i):
            c, i = c + i // TILES, i % TILES
            return c % 2, i // TT, i % TT

        def blocks(bank):
            return bank[:].rearrange("p (a t) -> p a t", a=TT)

        def apart(engine):
            engine.sem_inc(unused, 1)

        CHAIN = 3 + 4 * NEWTON

        block = keep.enter_context(nc.Block())

        @block.sync
        def _(sp):
            def load_x(b):
                sp.dma_start(x_rows[:], x[bass.ds(b * S, S), :].rearrange("(t p) c -> p t c", p=P)).then_inc(x_ld, 16)

            def load_ctx(b):
                sp.dma_start(cT_raw[:], ctxT[bass.ds(b * D, D), :].rearrange("(a p) t -> p a t", p=P)).then_inc(c_ld, 16)

            def load_w(n, w):
                sp.dma_start(pT[:, n, :, :], w.rearrange("(a p) e -> p a e", p=P)).then_inc(w_ld[n], 16)

            sp.dma_start(ident[:], ident_d).then_inc(ident_ld, 16)
            load_x(0)
            load_w(1, wk)
            load_ctx(0)
            for t, a in ((bq_col, bq), (bk_col, bk)):
                sp.dma_start(t[:], a).then_inc(bias_ld, 16)
            load_w(0, wq)
            load_w(2, wv)
            sp.dma_start(mask_u8, mask.rearrange("(t p) k -> p t k", p=P)).then_inc(mask_ld, 16)
            sp.dma_start(bv_row[:], bv.to_broadcast([P, D])).then_inc(bv_ld, 16)
            for t, a in ((mur_col, mur), (muk_col, muk)):
                sp.dma_start(t[:], a).then_inc(small_ld, 16)
            sp.dma_start(gates[:, 0:1], g_xattn.to_broadcast([P, 1])).then_inc(small_ld, 16)
            sp.dma_start(gates[:, 1:2], g_ffn.to_broadcast([P, 1])).then_inc(small_ld, 16)
            sp.dma_start(tgbo[:], bo.to_broadcast([P, D])).then_inc(small_ld, 16)

            def stack_rows(kind, n, bands, source, heads):
                dst = stack[n % 2]["QK".index(kind)]
                copied = stacked["QK".index(kind)]
                for j in heads:
                    for band in bands:
                        sp.dma_start(dst[HD * band:HD * (band + 1), j, :].bitcast(F32),
                                     source[HD * j:HD * (j + 1), :].bitcast(F32)).then_inc(copied[j], 16)

            def q_hi_count(b, n):
                return b * HI_PER_BATCH + HI_PROLOGUE if n == 1 else hi_no(b, ("Q", n)) + 1

            def q_lo_count(b, n):
                return done(b * SIDE_PER_BATCH + len(PROLOGUE) - 1) if n == 1 else done(side_no(b, ("Q", n)))

            def stack_q(b, n, heads):
                sp.wait_ge(side_hi, q_hi_count(b, n))
                apart(sp)
                stack_rows("Q", n, (0, 1), qk_hi[0], heads)
                sp.wait_ge(side_done, q_lo_count(b, n))
                apart(sp)
                stack_rows("Q", n, (2,), qk_lo[0], heads)

            def stack_k(b, n, heads):
                sp.wait_ge(side_done, done(side_no(b, ("K", n))))
                apart(sp)
                for j in heads:
                    stack_rows("K", n, (0, 2), qk_hi[1], (j,))
                    stack_rows("K", n, (1,), qk_lo[1], (j,))

            def stack_group(b, n):
                first = GH if n == GROUPS - 1 else GH - 1
                stack_q(b, n, range(first))
                stack_k(b, n, (0,))
                if first < GH:
                    stack_q(b, n, (first,))
                stack_k(b, n, range(1, GH))

            stack_k(None, 0, range(GH))
            for j in range(GH):
                stack_q(None, 0, (j,))

            def load_unit(b, h):
                sp.dma_start(c_raw[:, h], ctx_dram[bass.ds(b * D, D), :].rearrange("(a p) t -> p a t", p=P)[
                    :, :, h * UNIT:(h + 1) * UNIT]).then_inc(c2_ld[h], 16)
                sp.dma_start(x_in[:, h], x[bass.ds(b * S + h * UNIT, UNIT), :].rearrange(
                    "(m p) c -> p m c", p=P)).then_inc(x2_ld[h], 16)

            W2 = (wo, wkk, wr, wvv)

            def load_w2(n):
                if n >= 2:
                    sp.wait_ge(w2_lo_done[n - 2], 1)
                sp.dma_start(w2_raw[:, n % 2], W2[n].rearrange("(a p) e -> p a e", p=P)).then_inc(w2_ld[n % 2], 16)

            def store_context(b, c):
                sp.wait_ge(side_done, done(side_no(b, ("R", c))))
                apart(sp)
                sp.dma_start(ctx_dram[bass.ds(b * D + c * P, P), :], ctx_sb[:, c % 2, :]).then_inc(ctx_st[c % 2], 16)

            def batch(b):
                for c in range(GROUPS):
                    if c == 0 and not is_last(b):
                        sp.wait_ge(side_done, done(b * SIDE_PER_BATCH + len(PROLOGUE) - 1))
                        apart(sp)
                        load_x(b + 1)
                    if c:
                        store_context(b, c - 1)
                    if not (is_last(b) and c == GROUPS - 1):
                        sp.wait_ge(s_mm, tile_no(b, c, 0) + HEAD)
                        apart(sp)
                        if is_last(b) and c == GROUPS - 2:
                            sp.wait_ge(side_mm, mm_no(b, ("Q", c + 1)) + 1)
                            apart(sp)
                            load_w2(0)
                        stack_group(b, c + 1)
                    if c == 0 and not is_last(b):
                        load_ctx(b + 1)
                    if is_last(b) and c == GROUPS - 2:
                        load_unit(0, 0)
                        load_w2(1)
                        load_unit(0, 1)
                        load_w2(2)
                        load_w2(3)
                store_context(b, GROUPS - 1)

            with sp.Fori(0, B - 1) as b:
                batch(b)
            batch(B - 1)

            for s in range(2):
                sp.wait_ge(ctx_st[s], 16 * 2 * B + DMA_HEAD)

            def step2(b, h):
                if not is_last(b):
                    sp.wait_ge(c2_lo, b * 2 + h + 1)
                    apart(sp)
                    sp.wait_ge(x1_done, (b * 2 + h + 1) * UM)
                    apart(sp)
                    load_unit(b + 1, h)
                sp.wait_ge(o_done, b * 2 + h + 1 + HEAD)
                apart(sp)
                sp.dma_start(out[bass.ds(b * S + h * UNIT, UNIT), :].rearrange("(m p) c -> p m c", p=P),
                             o_sb[:, h]).then_inc(out_st[h], 16)

            with sp.Fori(0, B - 1) as b:
                step2(b, 0)
                step2(b, 1)
            step2(B - 1, 0)
            step2(B - 1, 1)
            for s in range(2):
                sp.wait_ge(out_st[s], 16 * B + DMA_HEAD)

        @block.tensor
        def _(pe):
            def one_term(part, dst, w_hi, w_lo, r_hi, r_lo, lhs, rhs):
                left, right = ((w_hi, r_lo), (w_lo, r_hi), (w_hi, r_hi))[part]
                for a in range(CH):
                    mm = nc.tensor.matmul(dst, lhs(left, a), rhs(right, a), start=(part == 0 and a == 0),
                                          stop=(part == TERMS - 1 and a == CH - 1))
                return mm

            def three_terms(*operands):
                for part in range(TERMS):
                    mm = one_term(part, *operands)
                return mm

            def side(b, kind, n, part, of):
                item = (kind, n)
                bank = side_bank_of(b, item)
                if kind == "C":
                    return
                if part == 0:
                    pe.wait_ge(side_done, side_no(b, item) + 1)
                if part == 0 and ((kind, n) in (("Q", 0), ("Q", 4), ("K", 0), ("K", 4)) or kind == "V" and n < 2):
                    pe.wait_ge(side_done, done(side_no(b, ("T", TT - 1) if kind == "Q" else ("C", CH - 1))))
                if kind == "T":
                    pe.wait_ge(xhat_done, (0 if b is None else b + 1) * TT + n + 1)
                    for a in range(CH):
                        mm = nc.tensor.transpose(bank[:, a * P:(a + 1) * P], x_rows[:, n, a * P:(a + 1) * P], ident[:])
                if kind in "QK":
                    which = "QK".index(kind)
                    cols = slice((n % 4) * P, (n % 4 + 1) * P)
                    w_hi, w_lo, r_hi, r_lo = w1_hi[which], w1_lo[which], act_hi[which], act_lo[which]
                    share = TERMS * CH // of
                    for at in range(part * share, (part + 1) * share):
                        left, right = ((w_hi, r_lo), (w_lo, r_hi), (w_hi, r_hi))[at // CH]
                        mm = nc.tensor.matmul(bank[:], left[:, at % CH, cols], right[:, at % CH, :],
                                              start=(at == 0), stop=(at == TERMS * CH - 1))
                if kind == "V":
                    share = 2 * TERMS * CH // of
                    for at in range(part * share, (part + 1) * share):
                        k, term, a = at // (TERMS * CH), at // CH % TERMS, at % CH
                        keys = 2 * (n % 2) + k
                        left, right = ((act_hi[1], w1_lo[2]), (act_lo[1], w1_hi[2]), (act_hi[1], w1_hi[2]))[term]
                        mm = nc.tensor.matmul(bank[:, k * UNIT:(k + 1) * UNIT], left[:, a, keys * P:(keys + 1) * P],
                                              right[:, a, n // 2 * UNIT:(n // 2 + 1) * UNIT],
                                              start=(term == 0 and a == 0), stop=(term == TERMS - 1 and a == CH - 1))
                if kind == "R":
                    pe.wait_ge(rden_ready, b * GROUPS + n + 1 + HEAD)
                    for q in range(TT):
                        mm = nc.tensor.transpose(bank[:, q * P:(q + 1) * P],
                                                 rden_rep[:, q].rearrange("p j d -> p (j d)"), ident[:])
                if part == of - 1:
                    mm.then_inc(side_mm, 1)

            def scores(b, c, i):
                slot, j, q = where(c, i)
                if i % TT == 0:
                    for copied in stacked:
                        pe.wait_ge(copied[j], (b * GROUPS + c + i // TILES + 1) * STACK_DMAS * 16)
                pe.wait_ge(s_min, tile_no(b, c, i) + 1)
                nc.tensor.matmul(s_bank[i % S_BANKS][:], stack[slot][0][:, j, q * P:(q + 1) * P],
                                 stack[slot][1][:, j, :], start=True, stop=True).then_inc(s_mm, 1)

            def transpose_probs(b, c, i):
                pe.wait_ge(p_exp, tile_no(b, c, i) + 1 + SM_RING)
                pe.wait_ge(pt_out[i % 2], b * (GROUPS * TILES // 2) + (c * TILES + i) // 2 + HEAD)
                for a in range(TT):
                    mm = nc.tensor.transpose(pt_bank[i % 2][:, a * P:(a + 1) * P],
                                             probs[:, i % P_RING, a * P:(a + 1) * P], ident[:])
                mm.then_inc(p_tr, 1)

            def context(b, c):
                for s in range(2):
                    pe.wait_ge(pt_out[s], (b * GROUPS + c + 1) * (TILES // 2) + HEAD)
                pe.wait_ge(side_done, previous_r(b, c))
                for a in range(TT):
                    for j in range(GH):
                        head = c * GH + j
                        nc.tensor.matmul(pv_bank[j * HD:(j + 1) * HD, :], v_sb[:, a, head * HD:(head + 1) * HD],
                                         pT[:, j, a, :], start=(a == 0), stop=(a == TT - 1))

            pe.wait_ge(ident_ld, 16)
            for kind, n in PROLOGUE:
                if (kind, n) == ("Q", 1):
                    scores(0, 0, 0)
                    scores(0, 0, 1)
                if kind in "KQV":
                    pe.wait_ge(w_lo_done, 1 + "KQV".index(kind))
                side(None, kind, n, 0, 1)
            scores(0, 0, 2)

            def batch(b):
                for c in range(GROUPS):
                    for i in range(TILES):
                        if i and not (is_last(b) and c == GROUPS - 1 and i + 2 >= TILES):
                            scores(b, c, i + 2)
                        for item in listed(PE_SIDE, b, c, i):
                            side(b, *item)
                        if is_last(b) and c == GROUPS - 1 and i in FIRST_O:
                            first_o_proj(FIRST_O.index(i))
                        transpose_probs(b, c, i)
                    for item in listed(PE_SIDE, b, c, TILES):
                        side(b, *item)
                    if is_last(b) and c == GROUPS - 1:
                        transposes(0, 0)
                    else:
                        scores(b, c, TILES + 2)
                    context(b, c)
                    side(b, "R", c, 0, 1)

            def first_o_proj(at):
                m, part = at // TERMS, at % TERMS
                if at == 0:
                    pe.wait_ge(w2_lo_done[0], 1)
                    pe.wait_ge(c2_lo, 1)
                    pe.wait_ge(side_done, done(side_no(B - 1, ("R", GROUPS - 2))))
                mm = one_term(part, o_bank[m][:], c_hi, c_lo, w2_hi[0], w2_lo[0],
                              lambda w, a: w[:, a, m * P:(m + 1) * P], lambda r, a: r[:, a, :])
                if part == TERMS - 1:
                    mm.then_inc(o_mm, 1)

            def transposes(b, h):
                u = b * 2 + h
                if isinstance(b, int) and b + h == 0:
                    pe.wait_ge(s_min, B * GROUPS * TILES + S_BANKS)
                else:
                    pe.wait_ge(kact_done, u * UM + HEAD)
                for m in range(UM):
                    pe.wait_ge(xh_done, u * UM + m + 1)
                    for a in range(CH):
                        mm = nc.tensor.transpose(k_bank[m][:, a * P:(a + 1) * P], xh[:, m, a * P:(a + 1) * P], ident[:])
                    mm.then_inc(t_mm, 1)

            with pe.Fori(0, B - 1) as b:
                batch(b)
            batch(B - 1)

            def o_proj(b, h):
                u = b * 2 + h
                pe.wait_ge(c2_lo, u + 1)
                pe.wait_ge(x1_done, u * UM)
                for m in range(UM):
                    three_terms(o_bank[m][:], c_hi, c_lo, w2_hi[0], w2_lo[0],
                                lambda w, a: w[:, a, m * P:(m + 1) * P], lambda r, a: r[:, a, :]).then_inc(o_mm, 1)

            def k_proj(b, h):
                pe.wait_ge(w2_lo_done[1], 1)
                pe.wait_ge(mixlo_done[0], b * 2 + h + 1)
                for m in range(UM):
                    for half in range(2):
                        n = 2 * m + half
                        mm = three_terms(k_bank[m][:, half * UNIT:(half + 1) * UNIT], w2_hi[1], w2_lo[1],
                                         mix_hi[0], mix_lo[0], lambda w, a: w[:, a, n * P:(n + 1) * P],
                                         lambda r, a: r[:, a, :])
                    mm.then_inc(k_mm, 1)

            def r_proj(b, h):
                u = b * 2 + h
                pe.wait_ge(w2_lo_done[2], 1)
                pe.wait_ge(mixlo_done[1], u + 1)
                pe.wait_ge(recept_done, u * UM + HEAD)
                for m in range(UM):
                    three_terms(r_bank[m][:], mix_hi[1], mix_lo[1], w2_hi[2], w2_lo[2],
                                lambda w, a: w[:, a, m * P:(m + 1) * P], lambda r, a: r[:, a, :]).then_inc(r_mm, 1)

            def v_proj(b, h):
                u = b * 2 + h
                pe.wait_ge(w2_lo_done[3], 1)
                pe.wait_ge(kactlo_done, u + 1 + HEAD)
                pe.wait_ge(y_done, u * UM + HEAD)
                for m in range(UM):
                    three_terms(v_bank[m][:], kact_hi, kact_lo, w2_hi[3], w2_lo[3],
                                lambda w, a: w[:, a, m * P:(m + 1) * P], lambda r, a: r[:, a, :]).then_inc(v_mm, 1)

            o_proj(0, 1)

            def step2(b, h):
                k_proj(b, h)
                r_proj(b, h)
                if h == 0:
                    transposes(b, 1)
                elif not is_last(b):
                    transposes(b + 1, 0)
                v_proj(b, h)
                if not is_last(b):
                    o_proj(b + 1, h)

            with pe.Fori(0, B - 1) as b:
                step2(b, 0)
                step2(b, 1)
            step2(B - 1, 0)
            step2(B - 1, 1)

        @block.scalar
        def _(act):
            def split_w(n):
                act.wait_ge(w_ld[n], 16)
                nc.scalar.mul(w1_hi[n][:], pT[:, n], -SCALE if n == 0 else 1.0).then_inc(w_hi_done, 1)

            def side(b, kind, n):
                item = (kind, n)
                bank = side_bank_of(b, item)
                if kind == "V":
                    return
                if kind in "QK" and not (b is None and n == 0):
                    for copied in stacked["QK".index(kind)]:
                        act.wait_ge(copied, ((0 if b is None else b * GROUPS) + n) * STACK_DMAS * 16)
                if kind == "R":
                    act.wait_ge(ctx_st[n % 2], (b * 2 + n // 2) * 16 + DMA_HEAD)
                if kind == "C":
                    if n == 0:
                        act.wait_ge(c_ld, (0 if b is None else b + 1) * 16 + 16)
                        if b is not None:
                            act.wait_ge(side_mm, mm_no(b, ("K", GROUPS - 1)) + 1)
                    nc.scalar.copy(act_hi[1][:, n, :], cT_raw[:, n, :]).then_inc(side_hi, 1)
                    return
                act.wait_ge(side_mm, mm_no(b, item) + 1)
                if kind == "T":
                    nc.scalar.copy(act_hi[0][:, :, n * P:(n + 1) * P], blocks(bank)).then_inc(side_hi, 1)
                if kind in "QK":
                    which = "QK".index(kind)
                    bias = (bq_neg, bk_col)[which][:, n % 4:n % 4 + 1]
                    nc.scalar.activation(qk_hi[which][:], bank[:], ACT.Identity, bias=bias).then_inc(side_hi, 1)
                if kind == "R":
                    nc.scalar.copy(ctx_sb[:, n % 2, :], bank[:]).then_inc(side_hi, 1)

            def exp(b, c, i):
                if i == TILES:
                    act.wait_ge(rden_ready, b * GROUPS + c + HEAD)
                act.wait_ge(s_min, tile_no(b, c, i) + 1 + S_BANKS)
                act.wait_ge(p_tr, tile_no(b, c, i) + 1)
                g = (c + i // TILES) % 2
                k = i % TILES
                nc.scalar.activation(probs[:, i % P_RING, :], neg_s[:, i % SM_RING, :], ACT.Exp,
                                     bias=negmax[:, k:k + 1], scale=-1.0,
                                     accum_out=den[:, g, k:k + 1]).then_inc(p_exp, 1)

            def probs_out(b, c, i):
                _, j, q = where(c, i)
                act.wait_ge(p_tr, tile_no(b, c, i) + 1 + P_RING)
                nc.scalar.copy(pT[:, j, :, q * P:(q + 1) * P], blocks(pt_bank[i % 2])).then_inc(pt_out[1], 1)

            split_w(1)
            for kind, n in PROLOGUE:
                if kind == "K":
                    act.wait_ge(bias_ld, 16 * 2)
                    nc.scalar.mul(bq_neg[:], bq_col[:], -SCALE).then_inc(consts, 1)
                    split_w(0)
                    split_w(2)
                if (kind, n) == ("Q", 1):
                    exp(0, 0, 0)
                if (kind, n) == ("Q", 0):
                    act.wait_ge(consts, 1)
                side(None, kind, n)
                if (kind, n) == ("Q", 0):
                    act.wait_ge(small_ld, 16 * 5)
                    nc.scalar.activation(tg[:], gates[:], ACT.Tanh).then_inc(consts, 1)

            def tile_step(b, c, i):
                for kind, n in listed(HI_SIDE, b, c, i):
                    side(b, kind, n)
                if not (is_last(b) and c == GROUPS - 1 and i + 1 >= TILES):
                    exp(b, c, i + 1)
                if i % 2:
                    probs_out(b, c, i)

            def early_steps(b):
                for i in range(EARLY):
                    tile_step(b, 0, i)
                    if i == HI_STEP and not isinstance(b, int):
                        side(b - 1, "R", GROUPS - 1)

            def batch(b):
                for c in range(GROUPS):
                    for i in range(EARLY if c == 0 else 0, TILES):
                        tile_step(b, c, i)
                        if is_last(b) and (c, i) in SPLIT_W2:
                            split_w2(SPLIT_W2.index((c, i)))
                        if is_last(b) and (c, i) == FIRST_CONTEXT:
                            context_hi(0, 0)
                    for kind, n in listed(HI_SIDE, b, c, END):
                        side(b, kind, n)
                    if is_last(b) and (c, END) in SPLIT_W2:
                        split_w2(SPLIT_W2.index((c, END)))
                    if is_last(b) and c == GROUPS - 1:
                        context_hi(0, 1)
                if not is_last(b):
                    early_steps(b + 1)

            def split_w2(n):
                act.wait_ge(w2_ld[n % 2], 16 * (n // 2 + 1))
                nc.scalar.copy(w2_hi[n][:], w2_raw[:, n % 2]).then_inc(w2_hi_done, 1)

            def context_hi(b, h):
                act.wait_ge(c2_ld[h], b * 16 + 16)
                if isinstance(b, int) and b + h == 0:
                    for copied in (*stacked[0], *stacked[1]):
                        act.wait_ge(copied, B * GROUPS * STACK_DMAS * 16)
                act.wait_ge(o_mm, (b * 2 + h) * UM)
                nc.scalar.copy(c_hi[:], c_raw[:, h]).then_inc(c2_hi, 1)

            early_steps(0)
            with act.Fori(0, B - 1) as b:
                batch(b)
            batch(B - 1)
            def xT_out(b, h):
                u = b * 2 + h
                if h == 1:
                    act.wait_ge(xT_done, u * UM)
                    nc.scalar.copy(xT[:, 1, :, 0:1], xT[:, 0, :, UNIT:UNIT + 1]).then_inc(carry_done, 1)
                for m in range(UM):
                    act.wait_ge(t_mm, u * UM + m + 1)
                    nc.scalar.copy(xT[:, h, :, 1 + m * P:1 + (m + 1) * P], blocks(k_bank[m])).then_inc(xT_done, 1)

            xT_out(0, 0)
            side(B - 1, "R", GROUPS - 1)

            def mixed_hi(b, h, n):
                act.wait_ge(mix_done[n], (b * 2 + h + 1) * CH)
                nc.scalar.copy(mix_hi[n][:], mix[n][:]).then_inc(mixhi_done[n], 1)

            def step2(b, h):
                u = b * 2 + h
                for m in range(UM):
                    act.wait_ge(kact_done, u * UM + HEAD)
                    act.wait_ge(k_mm, u * UM + m + 1)
                    nc.scalar.activation(relu[:, m], k_bank[m][:], ACT.Relu).then_inc(relu_done, 1)
                act.wait_ge(kact_done, (u + 1) * UM + HEAD)
                nc.scalar.copy(kact_hi[:].rearrange("p a t -> p (a t)"),
                               kact[:].rearrange("p m d -> p (m d)")).then_inc(kacthi_done, 1)
                if not is_last(b):
                    context_hi(b + 1, h)
                act.wait_ge(y_done, u * UM + HEAD)
                for m in range(UM):
                    act.wait_ge(r_mm, u * UM + m + 1)
                    nc.scalar.activation(recept[:, m], r_bank[m][:], ACT.Sigmoid).then_inc(recept_done, 1)
                if not (h and is_last(b)):
                    nb, nh = (b, 1) if h == 0 else (b + 1, 0)
                    xT_out(nb, nh)
                    mixed_hi(nb, nh, 0)
                    mixed_hi(nb, nh, 1)

            mixed_hi(0, 0, 0)
            mixed_hi(0, 0, 1)
            with act.Fori(0, B - 1) as b:
                step2(b, 0)
                step2(b, 1)
            step2(B - 1, 0)
            step2(B - 1, 1)

        @block.vector
        def _(dve):
            def split_w(n):
                dve.wait_ge(w_hi_done, 1 + (1, 0, 2).index(n))
                nc.vector.scalar_tensor_tensor(out=w1_lo[n][:], in0=pT[:, n], scalar=-SCALE if n == 0 else 1.0,
                                               in1=w1_hi[n][:], op0=ALU.mult, op1=ALU.subtract).then_inc(w_lo_done, 1)

            def row_stats(b, t):
                if t == 0:
                    dve.wait_ge(x_ld, b * 16 + 16)
                    dve.wait_ge(mv_done, b * TT)
                nc.vector.bn_stats(stats[:, t, :], x_rows[:, t, :]).then_inc(bn_done, 1)

            def mean_and_variance(b):
                dve.wait_ge(xhat_done, b * TT)
                for t in range(TT):
                    dve.wait_ge(bn_done, b * TT + t + 1)
                    apart(dve)
                    nc.vector.bn_aggr(mv[:, t, :], stats[:, t, :]).then_inc(mv_done, 1)

            def side(b, kind, n):
                item = (kind, n)
                bank = side_bank_of(b, item)
                if kind == "V":
                    dve.wait_ge(side_mm, mm_no(b, item) + 1)
                    cols = slice(n // 2 * UNIT, (n // 2 + 1) * UNIT)
                    nc.vector.tensor_tensor(v_sb[:, 2 * (n % 2):2 * (n % 2) + 2, cols],
                                            bank[:].rearrange("p (k e) -> p k e", k=2),
                                            bv_row[:, None, cols].to_broadcast([P, 2, UNIT]), ALU.add).then_inc(side_done, 1)
                    return
                dve.wait_ge(side_hi, hi_no(b, item) + 1)
                if kind == "C":
                    nc.vector.tensor_tensor(act_lo[1][:, n, :], cT_raw[:, n, :], act_hi[1][:, n, :],
                                            ALU.subtract).then_inc(side_done, 1)
                if kind == "T":
                    t = slice(n * P, (n + 1) * P)
                    nc.vector.tensor_tensor(act_lo[0][:, :, t], blocks(bank), act_hi[0][:, :, t],
                                            ALU.subtract).then_inc(side_done, 1)
                if kind in "QK":
                    which = "QK".index(kind)
                    bias = (bq_neg, bk_col)[which][:, n % 4:n % 4 + 1]
                    nc.vector.scalar_tensor_tensor(out=qk_lo[which][:], in0=bank[:], scalar=bias, in1=qk_hi[which][:],
                                                   op0=ALU.add, op1=ALU.subtract).then_inc(side_done, 1)
                if kind == "R":
                    nc.vector.tensor_tensor(ctx_sb[:, n % 2, :], pv_bank[:], ctx_sb[:, n % 2, :],
                                            ALU.mult).then_inc(side_done, 1)

            def mask_and_min(b, c, i):
                _, _, q = where(c, i)
                k = i % TILES
                dve.wait_ge(s_mm, tile_no(b, c, i) + 1 + HEAD)
                dve.wait_ge(p_exp, tile_no(b, c, i) + 1)
                apart(dve)
                nc.vector.tensor_tensor_reduce(neg_s[:, i % SM_RING, :], s_bank[i % S_BANKS][:], mask_big[:, q, :], 1.0,
                                               3e38, ALU.add, ALU.min, negmax[:, k:k + 1]).then_inc(s_min, 1)

            def probs_out(b, c, i):
                _, j, q = where(c, i)
                dve.wait_ge(p_tr, tile_no(b, c, i) + 1 + P_RING)
                nc.vector.tensor_copy(pT[:, j, :, q * P:(q + 1) * P], blocks(pt_bank[i % 2])).then_inc(pt_out[0], 1)

            def reciprocals(b, c):
                g = b * GROUPS + c
                dve.wait_ge(p_exp, (g + 1) * TILES + SM_RING)
                dve.wait_ge(rden_ready, g + HEAD)
                nc.vector.reciprocal(rden[:], den[:, c % 2, :]).then_inc(rden_calc, 1)
                dve.wait_ge(rden_calc, g + 1)
                src = rden[:].rearrange("p (j q) -> p q j", j=GH)[:, :, :, None].to_broadcast([P, TT, GH, HD])
                nc.vector.tensor_copy(rden_rep[:], src).then_inc(rden_ready, 1)

            for t in range(TT):
                row_stats(0, t)
            mean_and_variance(0)
            split_w(1)
            for kind, n in PROLOGUE:
                if kind == "K":
                    dve.wait_ge(pool_chain, CHAIN)
                    for t in range(TT):
                        nc.vector.tensor_scalar(x_rows[:, t, :], x_rows[:, t, :], mv[:, t, 0:1], rstd[:, t:t + 1],
                                                ALU.subtract, ALU.mult).then_inc(xhat_done, 1)
                    split_w(0)
                if (kind, n) == ("Q", 1):
                    dve.wait_ge(mask_done, 1)
                    mask_and_min(0, 0, 0)
                    mask_and_min(0, 0, 1)
                if (kind, n) == ("Q", 0):
                    split_w(2)
                    dve.wait_ge(consts, 1)
                side(None, kind, n)
                if (kind, n) == ("Q", 0):
                    dve.wait_ge(mask_ld, 16)
                    nc.vector.tensor_scalar(mask_big[:], mask_u8, MASKED, None, ALU.mult).then_inc(mask_done, 1)
                    dve.wait_ge(bv_ld, 16)
            dve.wait_ge(consts, 2)
            nc.vector.tensor_scalar(tgbo[:], tgbo[:], tg[:, 0:1], None, ALU.mult).then_inc(consts, 1)

            def tile_step(b, c, i):
                for kind, n in listed(LO_SIDE, b, c, i):
                    side(b, kind, n)
                if not (is_last(b) and c == GROUPS - 1 and i + 2 >= TILES):
                    mask_and_min(b, c, i + 2)
                if i % 2 == 0:
                    probs_out(b, c, i)

            def early_steps(b):
                for i in range(EARLY):
                    tile_step(b, 0, i)
                    if i == LO_STEP and not isinstance(b, int):
                        side(b - 1, "R", GROUPS - 1)

            def batch(b):
                for c in range(GROUPS):
                    for i in range(EARLY if c == 0 else 0, TILES):
                        tile_step(b, c, i)
                        if c == 0 and i in STATS_STEPS and not is_last(b):
                            row_stats(b + 1, STATS_STEPS.index(i))
                            if i == STATS_STEPS[-1]:
                                mean_and_variance(b + 1)
                        if is_last(b) and (c, i) == FIRST_CONTEXT:
                            context_lo(0, 0)
                        if is_last(b) and (c, i) == FIRST_RESIDUAL:
                            residual1(0, 0)
                        if is_last(b) and (c, i) == FIRST_NORM:
                            normalise2(0, 0)
                    reciprocals(b, c)
                    if is_last(b) and c == GROUPS - 2:
                        dve.wait_ge(w2_hi_done, 1)
                        nc.vector.tensor_tensor(w2_lo[0][:], w2_raw[:, 0], w2_hi[0][:],
                                                ALU.subtract).then_inc(w2_lo_done[0], 1)
                    if is_last(b) and c == GROUPS - 1:
                        context_lo(0, 1)
                    for kind, n in listed(LO_SIDE, b, c, END):
                        side(b, kind, n)
                if not is_last(b):
                    early_steps(b + 1)

            def context_lo(b, h):
                dve.wait_ge(c2_hi, b * 2 + h + 1)
                nc.vector.tensor_tensor(c_lo[:], c_raw[:, h], c_hi[:], ALU.subtract).then_inc(c2_lo, 1)

            def residual1(b, h):
                u = b * 2 + h
                dve.wait_ge(xb_done, u + 1)
                if isinstance(b, int) and b + h == 0:
                    dve.wait_ge(consts, 3)
                if not (isinstance(b, int) and b == 0):
                    dve.wait_ge(o_done, u - 1 + HEAD)
                for m in range(UM):
                    dve.wait_ge(o_mm, u * UM + m + 1)
                    nc.vector.scalar_tensor_tensor(out=x1[:, h, m], in0=o_bank[m][:], scalar=tg[:, 0:1],
                                                   in1=x_in[:, h, m], op0=ALU.mult, op1=ALU.add).then_inc(x1_done, 1)
                dve.wait_ge(mv2_done, u * UM)
                dve.wait_ge(xh_done, u * UM)
                for m in range(UM):
                    dve.wait_ge(x1_done, u * UM + m + 1)
                    nc.vector.bn_stats(stats2[:, m, :], x1[:, h, m]).then_inc(bn2_done, 1)
                for m in range(UM):
                    dve.wait_ge(bn2_done, u * UM + m + 1)
                    apart(dve)
                    nc.vector.bn_aggr(mv2[:, m, :], stats2[:, m, :]).then_inc(mv2_done, 1)

            def normalise2(b, h):
                u = b * 2 + h
                dve.wait_ge(pool_chain2, (u + 1) * CHAIN)
                dve.wait_ge(t_mm, u * UM)
                for m in range(UM):
                    nc.vector.tensor_scalar(xh[:, m], x1[:, h, m], mv2[:, m, 0:1], rstd2[:, m:m + 1],
                                            ALU.subtract, ALU.mult).then_inc(xh_done, 1)

            early_steps(0)
            with dve.Fori(0, B - 1) as b:
                batch(b)
            batch(B - 1)
            def difference(b, h):
                u = b * 2 + h
                dve.wait_ge(xT_done, (u + 1) * UM)
                if h == 1:
                    dve.wait_ge(carry_done, b + 1)
                dve.wait_ge(mix_done[1], u * CH)
                nc.vector.tensor_tensor(diff[:], xT[:, h, :, 1:1 + UNIT], xT[:, h, :, 0:UNIT],
                                        ALU.subtract).then_inc(diff_done, 1)
                dve.wait_ge(diff_done, u + 1)

            def mixed(b, h, n):
                dve.wait_ge(mixlo_done[n], b * 2 + h)
                for a in range(CH):
                    nc.vector.scalar_tensor_tensor(out=mix[n][:, a], in0=diff[:, a],
                                                   scalar=(muk_col, mur_col)[n][:, a:a + 1],
                                                   in1=xT[:, h, a, 0:UNIT], op0=ALU.mult,
                                                   op1=ALU.add).then_inc(mix_done[n], 1)

            def mixed_lo(b, h, n):
                dve.wait_ge(mixhi_done[n], b * 2 + h + 1)
                nc.vector.tensor_tensor(mix_lo[n][:], mix[n][:], mix_hi[n][:], ALU.subtract).then_inc(mixlo_done[n], 1)

            def step2(b, h):
                u = b * 2 + h
                more = not (h and is_last(b))
                nb, nh = (b, 1) if h == 0 else (b + 1, 0)
                if more:
                    residual1(nb, nh)
                mixed_lo(b, h, 1)
                dve.wait_ge(kactlo_done, u + HEAD)
                for m in range(UM):
                    dve.wait_ge(relu_done, u * UM + m + 1)
                    nc.vector.scalar_tensor_tensor(out=kact[:, m], in0=k_bank[m][:], scalar=0.0, in1=relu[:, m],
                                                   op0=ALU.max, op1=ALU.mult).then_inc(kact_done, 1)
                dve.wait_ge(kacthi_done, u + 1)
                nc.vector.tensor_tensor(kact_lo[:].rearrange("p a t -> p (a t)"), kact[:].rearrange("p m d -> p (m d)"),
                                        kact_hi[:].rearrange("p a t -> p (a t)"), ALU.subtract).then_inc(kactlo_done, 1)
                if more:
                    normalise2(nb, nh)
                if not is_last(b):
                    context_lo(b + 1, h)
                if more:
                    difference(nb, nh)
                    mixed(nb, nh, 0)
                    mixed(nb, nh, 1)
                    mixed_lo(nb, nh, 0)
                dve.wait_ge(out_st[h], b * 16 + DMA_HEAD)
                for m in range(UM):
                    dve.wait_ge(v_mm, u * UM + m + 1)
                    dve.wait_ge(recept_done, u * UM + m + 1 + HEAD)
                    nc.vector.scalar_tensor_tensor(out=o_sb[:, h, m], in0=v_bank[m][:], scalar=tg[:, 1:2],
                                                   in1=recept[:, m], op0=ALU.mult, op1=ALU.mult).then_inc(y_done, 1)

            nc.vector.memset(xT[:, 0, :, 0:1], 0.0).then_inc(mask_done, 1)
            dve.wait_ge(mask_done, 2)
            difference(0, 0)
            mixed(0, 0, 0)
            side(B - 1, "R", GROUPS - 1)
            mixed(0, 0, 1)
            mixed_lo(0, 0, 0)
            with dve.Fori(0, B - 1) as b:
                step2(b, 0)
                step2(b, 1)
            step2(B - 1, 0)
            step2(B - 1, 1)

        @block.gpsimd
        def _(pool):
            for ring, length in ((side_done, SIDE_BANKS), (s_min, S_BANKS), (p_exp, SM_RING), (p_tr, P_RING)):
                pool.sem_inc(ring, length)
            for signal in (s_mm, *pt_out, rden_ready, kact_done, y_done, recept_done, kactlo_done, o_done):
                pool.sem_inc(signal, HEAD)
            for signal in (*ctx_st, *out_st):
                pool.sem_inc(signal, DMA_HEAD)
            def inverse_root(base, sem_, var, ve, y, t):
                n = [0]

                def link(ins):
                    n[0] += 1
                    ins.then_inc(sem_, 1)
                    pool.wait_ge(sem_, base + n[0])
                    apart(pool)

                link(nc.gpsimd.tensor_scalar(ve, var, EPS, None, ALU.add))
                link(nc.gpsimd.tensor_scalar(t.bitcast(I32), ve.bitcast(I32), -0.5, RSQRT_MAGIC, ALU.mult, ALU.add))
                link(nc.gpsimd.tensor_copy(y, t))
                for _ in range(NEWTON):
                    link(nc.gpsimd.tensor_tensor(t, y, y, ALU.mult))
                    link(nc.gpsimd.tensor_tensor(t, t, ve, ALU.mult))
                    link(nc.gpsimd.tensor_scalar(t, t, -0.5, 1.5, ALU.mult, ALU.add))
                    link(nc.gpsimd.tensor_tensor(y, y, t, ALU.mult))

            def normalise(b):
                pool.wait_ge(mv_done, (b + 1) * TT)
                apart(pool)
                inverse_root(b * CHAIN, pool_chain, mv[:, :, 1], var_eps[:], rstd[:], newton[:])
                if isinstance(b, int):
                    return
                for t in range(TT):
                    nc.gpsimd.tensor_scalar(x_rows[:, t, :], x_rows[:, t, :], mv[:, t, 0:1], rstd[:, t:t + 1],
                                            ALU.subtract, ALU.mult).then_inc(xhat_done, 1)

            normalise(0)
            with pool.Fori(0, B - 1) as b:
                normalise(b + 1)

            def add_bias(b, h):
                pool.wait_ge(x2_ld[h], b * 16 + 16)
                nc.gpsimd.tensor_tensor(x_in[:, h], x_in[:, h], tgbo[:, None, :].to_broadcast([P, UM, D]),
                                        ALU.add).then_inc(xb_done, 1)

            def inverse_root2(b, h):
                u = b * 2 + h
                pool.wait_ge(mv2_done, (u + 1) * UM)
                apart(pool)
                inverse_root(u * CHAIN, pool_chain2, mv2[:, :, 1], var_eps2[:], rstd2[:], newton2[:])

            def step2(b, h):
                u = b * 2 + h
                if not (h and is_last(b)):
                    inverse_root2(*((b, 1) if h == 0 else (b + 1, 0)))
                if not is_last(b):
                    add_bias(b + 1, h)
                pool.wait_ge(y_done, (u + 1) * UM + HEAD)
                nc.gpsimd.tensor_tensor(o_sb[:, h], o_sb[:, h], x1[:, h], ALU.add).then_inc(o_done, 1)

            def split_w2(n):
                pool.wait_ge(w2_hi_done, n + 1)
                nc.gpsimd.tensor_tensor(w2_lo[n][:], w2_raw[:, n % 2], w2_hi[n][:], ALU.subtract).then_inc(w2_lo_done[n], 1)

            pool.wait_ge(consts, 3)
            add_bias(0, 0)
            split_w2(1)
            inverse_root2(0, 0)
            split_w2(2)
            add_bias(0, 1)
            split_w2(3)
            with pool.Fori(0, B - 1) as b:
                step2(b, 0)
                step2(b, 1)
            step2(B - 1, 0)
            step2(B - 1, 1)


def kernel(x, ctx_1024, mask_SxS2_bk1, g_xattn, g_ffn, L0_xattn_q_w, L0_xattn_q_b, L0_xattn_k_w, L0_xattn_k_b,
           L0_xattn_v_w, L0_xattn_v_b, L0_xattn_o_w, L0_xattn_o_b, L0_ffn_W_r, L0_ffn_W_k, L0_ffn_W_v, L0_ffn_mu_r,
           L0_ffn_mu_k):
    import numpy as np
    import concourse.bacc as bacc
    from concourse.bass_utils import run_bass_kernel_spmd

    def turned(w):
        return np.ascontiguousarray(np.asarray(w).T)

    def columns(v):
        return np.ascontiguousarray(np.asarray(v).reshape(CH, P).T)

    def row(v):
        return np.asarray(v).reshape(1, -1)

    arrays = {
        "x": np.asarray(x).reshape(B * S, D),
        "ctxT": np.ascontiguousarray(np.asarray(ctx_1024).transpose(0, 2, 1)).reshape(B * D, S),
        "mask": np.asarray(mask_SxS2_bk1),
        "g_xattn": row(g_xattn), "g_ffn": row(g_ffn),
        "wqT": turned(L0_xattn_q_w), "bq": columns(L0_xattn_q_b),
        "wkT": turned(L0_xattn_k_w), "bk": columns(L0_xattn_k_b),
        "wvT": turned(L0_xattn_v_w), "bv": row(L0_xattn_v_b),
        "woT": turned(L0_xattn_o_w), "bo": row(L0_xattn_o_b),
        "wrT": turned(L0_ffn_W_r), "wkkT": turned(L0_ffn_W_k), "wvvT": turned(L0_ffn_W_v),
        "mur": columns(L0_ffn_mu_r), "muk": columns(L0_ffn_mu_k),
        "ident_d": np.eye(P, dtype=np.float32),
    }
    nc = bacc.Bacc("TRN2", target_bir_lowering=False, num_devices=1)
    args = [nc.dram_tensor(name, a.shape, mybir.dt.from_np(a.dtype), kind="ExternalInput").ap()
            for name, a in arrays.items()]
    out = nc.dram_tensor("out", (B * S, D), F32, kind="ExternalOutput").ap()
    ctx_dram = nc.dram_tensor("ctx_dram", (B * D, S), F32, kind="Internal").ap()
    build(nc, *args, out, ctx_dram)
    result = run_bass_kernel_spmd(nc, [arrays], core_ids=[0])
    return result.results[0]["out"].reshape(B, S, D)
```
